# Optimizing a Trainium2 kernel written in Bass

```python
import numpy as np
import jax
import jax.numpy as jnp

def _softmax(x, axis=-1):
    return jax.nn.softmax(x, axis=axis)

def _gelu(x):
    return jax.nn.gelu(x, approximate=True)

def _silu(x):
    return jax.nn.silu(x)

def _sigmoid(x):
    return jax.nn.sigmoid(x)

def _layernorm(x, axis=-1, eps=1e-05):
    m = jnp.mean(x, axis=axis, keepdims=True)
    v = jnp.var(x, axis=axis, keepdims=True)
    return (x - m) / jnp.sqrt(v + eps)

def _scatter_add(tgt, idx, src, axis=0):
    return tgt.at[idx].add(src)

def _segment_sum(src, seg, n):
    return jax.ops.segment_sum(src, seg, n)
kernel_name = 'mk_gnn_ffn_d1_gnn_r32_23bcab'

def setup_inputs(seed: int=0):
    np.random.seed(seed)
    _w = jnp.asarray

    def _rec_inputs():
        import jax
        import jax.numpy as jnp
        _gk = jax.random.key(seed)
        x = -0.0001126 + 1 * jax.random.normal(jax.random.fold_in(_gk, 1), (10000, 768), jnp.float32)
        src = jax.random.randint(jax.random.fold_in(_gk, 2), (5000,), 0, 10000, jnp.int32)
        dst = jnp.minimum((10000 * jax.random.uniform(jax.random.fold_in(_gk, 3), (5000,)) ** 2.0).astype(jnp.int32), 9999)
        _o = jnp.argsort(dst, stable=True)
        src = src[_o]
        dst = dst[_o]
        return (x, src, dst)
    x, src, dst = _rec_inputs()

    def _L0_gnn_setup():
        import jax, jax.numpy as jnp
        import numpy as np
        N_NODES = 10000
        N_EDGES = 3125
        DIM = 768
        key = jax.random.key(seed)
        k1, k2, k3, k4 = jax.random.split(key, 4)
        x = jax.random.normal(k1, (N_NODES, DIM), dtype=jnp.float32)
        edge_index = jax.random.randint(k2, (2, N_EDGES), 0, N_NODES, dtype=jnp.int32)
        W = jax.random.normal(k3, (DIM, DIM), dtype=jnp.float32) / np.sqrt(DIM)
        b = jnp.zeros((DIM,), dtype=jnp.float32)
        return {'x': x, 'edge_index': edge_index, 'W': W, 'b': b}
    _L0_gnn_all = _L0_gnn_setup()
    _L0_gnn_in = {k: v for k, v in _L0_gnn_all.items() if k in ('W', 'b')}
    del _L0_gnn_all

    def _L0_ffn_setup():
        import jax, jax.numpy as jnp
        import numpy as np
        B, T, C = (2, 1024, 768)
        H, NE, K = (96, 8, 2)
        key = jax.random.key(seed)
        k1, k2, k3, k4 = jax.random.split(key, 4)
        x = jax.random.normal(k1, (B, T, C), dtype=jnp.float32)
        w_fc = jax.random.normal(k2, (C, H * NE), dtype=jnp.float32) * 0.02
        w_proj = jax.random.normal(k3, (H * NE, C), dtype=jnp.float32) * (0.02 * (2 * 12) ** (-0.5))
        w_gate = jax.random.normal(k4, (C, NE), dtype=jnp.float32) * 0.02
        return {'x': x, 'w_fc': w_fc, 'w_proj': w_proj, 'w_gate': w_gate}
    _L0_ffn_all = _L0_ffn_setup()
    _L0_ffn_in = {k: v for k, v in _L0_ffn_all.items() if k in ('w_fc', 'w_proj', 'w_gate')}
    del _L0_ffn_all
    return {'x': x, 'src': src, 'dst': dst, 'L0_gnn_W': _L0_gnn_in['W'], 'L0_gnn_b': _L0_gnn_in['b'], 'L0_ffn_w_fc': _L0_ffn_in['w_fc'], 'L0_ffn_w_proj': _L0_ffn_in['w_proj'], 'L0_ffn_w_gate': _L0_ffn_in['w_gate']}

def reference(x, src, dst, L0_gnn_W, L0_gnn_b, L0_ffn_w_fc, L0_ffn_w_proj, L0_ffn_w_gate):
    import jax
    import jax.numpy as jnp

    def _L0_gnn_ref(x, edge_index, W, b):
        import jax, jax.numpy as jnp
        import numpy as np
        N_NODES = 10000
        N_EDGES = 3125
        DIM = 768
        n = x.shape[0]
        loop = jnp.arange(n, dtype=edge_index.dtype)
        src = jnp.concatenate([edge_index[0], loop])
        dst = jnp.concatenate([edge_index[1], loop])
        deg = jax.ops.segment_sum(jnp.ones_like(dst, dtype=x.dtype), dst, num_segments=n)
        deg_inv_sqrt = jnp.where(deg > 0, jax.lax.rsqrt(deg), 0.0)
        norm = deg_inv_sqrt[src] * deg_inv_sqrt[dst]
        h = x @ W
        msg = h[src] * norm[:, None]
        out = jax.ops.segment_sum(msg, dst, num_segments=n)
        return out + b

    def _L0_ffn_ref(x, w_fc, w_proj, w_gate):
        import jax, jax.numpy as jnp
        import numpy as np
        B, T, C = (2, 1024, 768)
        H, NE, K = (96, 8, 2)
        router_logits = jnp.einsum('btc,ce->bte', x, w_gate)
        router_probs = jax.nn.softmax(router_logits, axis=-1)
        top_p, top_i = jax.lax.top_k(router_probs, K)
        top_p = top_p / jnp.sum(top_p, axis=-1, keepdims=True)
        wf = w_fc.reshape(C, H, NE)
        h_all = jnp.einsum('btc,che->bthe', x, wf)
        h = jnp.take_along_axis(h_all, top_i[:, :, None, :], axis=-1)
        h = jax.nn.gelu(h, approximate=True)
        wp = w_proj.reshape(H, C, NE)
        o_all = jnp.einsum('bthk,hce->btcke', h, wp)
        o = jnp.take_along_axis(o_all, top_i[:, :, None, :, None], axis=-1)[..., 0]
        o = jnp.einsum('btck,btk->btc', o, top_p)
        return o
    edge_index = jnp.stack([src, dst])
    x = x + _L0_gnn_ref(_layernorm(x, axis=-1), edge_index, L0_gnn_W, L0_gnn_b)
    x = x + _L0_ffn_ref(_layernorm(x, axis=-1)[None], L0_ffn_w_fc, L0_ffn_w_proj, L0_ffn_w_gate)[0]
    return x

_drawn_inputs = setup_inputs


def setup_inputs(seed=0):
    import zlib

    import numpy as np

    out = dict(_drawn_inputs(seed))
    spreads = {'L0_gnn_b': (0.0, 0.1)}
    factors = {'L0_ffn_w_fc': 8.0, 'L0_ffn_w_proj': 8.0, 'L0_ffn_w_gate': 8.0}
    for name, (base, spread) in spreads.items():
        noise = np.random.default_rng([zlib.crc32(name.encode()), seed]).standard_normal(out[name].shape)
        drawn = base * np.exp(spread * noise) if base else spread * noise
        out[name] = jnp.asarray(drawn.astype(out[name].dtype))
    for name, factor in factors.items():
        out[name] = (out[name] * factor).astype(out[name].dtype)
    return out
```

```python
import concourse.bass as bass
from concourse import mybir
from contextlib import ExitStack


def gnn_moe_ffn_kernel(nc, x, src, dst, w_gnn, b_gnn, w_fc, w_proj, w_gate, out, dinv_dram, list_dram):
    F32, F16, I32 = mybir.dt.float32, mybir.dt.float16, mybir.dt.int32
    ALU, ACT, AX = mybir.AluOpType, mybir.ActivationFunctionType, mybir.AxisListType

    N, D = x.shape
    E = src.shape[0]
    NE = w_gate.shape[1]
    P = 128
    M = 125
    TILES = N // M
    GT = 4
    GROUPS = TILES // GT
    KC = D // P
    HALF = D // 2
    EP, EC = 125, E // 125
    WIN = P
    ROUNDS = -(-E // WIN)
    SLOTS = ROUNDS * WIN
    SRC_LO = 128
    EPS = 1e-5
    XS_LOG = 4
    XS = float(2 ** XS_LOG)
    W_LOG = 12
    RSQRT_MAGIC = 0x5F3759DF
    OV_STEPS = 16

    x_t = x.rearrange("(p t) d -> p t d", t=TILES)
    out_t = out.rearrange("(p t) d -> p t d", t=TILES)

    ctx = ExitStack()
    with ctx:
        def sb(name, shape, dt, c=ctx):
            return c.enter_context(nc.sbuf_tensor(name, shape, dt))

        def sem(name):
            return ctx.enter_context(nc.semaphore(name))

        w_hi = [sb(f"w_hi_{n}", [P, KC, D], F16) for n in ("gnn", "fc", "proj")]
        w_lo = [sb(f"w_lo_{n}", [P, KC, D], F16) for n in ("gnn", "fc", "proj")]
        gate = sb("gate", [P, KC, 2 * NE], F16)
        ident16 = sb("ident16", [P, P], F16)
        ident = sb("ident", [P, P], F32)
        iota_row = sb("iota_row", [P, P], F32)
        iota_row_i = sb("iota_row_i", [P, P], I32)
        iota_part_i = sb("iota_part_i", [P, 1], I32)
        iota_part = sb("iota_part", [P, 1], F32)
        rank8 = sb("rank8", [P, NE], F32)
        bias_row = sb("bias_row", [P, D], F32)
        scales = sb("scales", [P, 12], F32)
        inv_gnn, inv_fc, inv_gate, inv_out, v_scale = (scales[:, i:i + 1] for i in range(5))
        deg_inv = sb("deg_inv", [P, TILES], F32)
        win_src = sb("win_src", [P, TILES], I32)
        win_dst = sb("win_dst", [P, TILES], I32)
        win_b = sb("win_b", [P, TILES], F32)

        pad_p = sb("pad_p", [1, 1], F32)
        most = sb("most", [1, 1], I32)

        ps_t = ctx.enter_context(nc.psum_tensor("ps_t", [P, 2, 512], F32))
        ps_y = ctx.enter_context(nc.psum_tensor("ps_y", [P, 2, 512], F32))
        ps_d = ctx.enter_context(nc.psum_tensor("ps_d", [P, 2, 512], F32))
        ps_u = [ctx.enter_context(nc.psum_tensor(f"ps_u{i}", [P, 512], F32)) for i in range(2)]

        prep = ExitStack()
        stage = [sb(f"stage_{n}", [P, KC, D], F32, prep) for n in ("gnn", "fc", "proj")]
        gate_f = sb("gate_f", [P, KC, NE], F32, prep)
        wmax = sb("wmax", [P, 4], F32, prep)
        wabs = sb("wabs", [P, 4], F32, prep)
        wexp = sb("wexp", [P, 4], I32, prep)
        wscale = sb("wscale", [P, 4], F32, prep)
        wun = sb("wun", [P, 4], F32, prep)
        src_i = sb("src_i", [EP, EC], I32, prep)
        dst_i = sb("dst_i", [EP, EC], I32, prep)
        q_i = sb("q_i", [EP, 2, EC], I32, prep)
        ed = sb("ed", [EP, 10, EC], F32, prep)
        src_f, dst_f, hi_f, lo_f, q_f, r_f, neg_f, a_f, b1_f, rank_f = (ed[:, i, :] for i in range(10))
        oh_a = sb("oh_a", [EP, EC, TILES], F16, prep)
        oh_b = sb("oh_b", [EP, EC, M], F16, prep)
        cum = sb("cum", [EP, EC + 1, TILES], F16, prep)
        before = sb("before", [EP, EP], F16, prep)
        ones16 = sb("ones16", [EP, EP], F16, prep)
        picked = sb("picked", [EP, 6, TILES], F32, prep)
        oh_r = sb("oh_r", [EP, EC, WIN], F16, prep)
        vals = sb("vals", [EP, EC, 3, TILES], F16, prep)
        pos_i = sb("pos_i", [EP, EC], I32, prep)
        row_i = sb("row_i", [EP, EC, 3], I32, prep)
        fill = sb("fill", [P, TILES, 3], I32, prep)
        pos_c = sb("pos_c", [EP, 1], I32, prep)
        row_c = sb("row_c", [EP, 3], I32, prep)
        lists = sb("lists", [P, 3, TILES], F32, prep)
        tmp_w = sb("tmp_w", [P, 2, TILES], F32, prep)
        newton = sb("newton", [P, 3, TILES], F32, prep)

        s_edges = sem("s_edges")
        s_w = [sem(f"s_w{i}") for i in range(4)]
        s_bias = sem("s_bias")
        s_iota = sem("s_iota")
        s_const = sem("s_const")
        s_oh = sem("s_oh")
        s_cum = sem("s_cum")
        s_count = sem("s_count")
        s_rank_mm = sem("s_rank_mm")
        s_rank_used = sem("s_rank_used")
        s_vals = sem("s_vals")
        s_lists = sem("s_lists")
        s_total = sem("s_total")
        s_most = sem("s_most")
        s_fill0 = sem("s_fill0")
        s_fill = sem("s_fill")
        s_col = sem("s_col")
        s_scatter = sem("s_scatter")
        s_dinv = sem("s_dinv")
        s_dinv_st = sem("s_dinv_st")
        s_wmax = sem("s_wmax")
        s_wabs = sem("s_wabs")
        s_wscale = sem("s_wscale")
        s_whi = sem("s_whi")
        s_chain = sem("s_chain")
        RB = 6
        RBATCH = -(-EC // RB)

        with nc.Block() as block:
            @block.sync
            def _(sp):
                sp.dma_start(src_i[:], src.rearrange("(p c) -> p c", p=EP)).then_inc(s_edges, 16)
                sp.dma_start(dst_i[:], dst.rearrange("(p c) -> p c", p=EP)).then_inc(s_edges, 16)
                for i, w in enumerate((w_gnn, w_fc, w_proj)):
                    sp.dma_start(stage[i][:], w.rearrange("(c p) n -> p c n", p=P)).then_inc(s_w[i], 16)
                sp.dma_start(gate_f[:], w_gate.rearrange("(c p) n -> p c n", p=P)).then_inc(s_w[3], 16)
                sp.dma_start(bias_row[:], b_gnn.partition_broadcast(P)).then_inc(s_bias, 16)
                sp.wait_ge(s_dinv, 1)
                sp.dma_start(dinv_dram.rearrange("(p t) o -> p (t o)", t=TILES),
                             newton[0:M, 0, :]).then_inc(s_dinv_st, 16)
                sp.wait_ge(s_dinv_st, 16)
                sp.wait_ge(s_bias, 16)

            @block.gpsimd
            def _(pool):
                nc.gpsimd.iota(iota_row_i[:], [[1, P]], base=0, channel_multiplier=0)
                nc.gpsimd.iota(iota_part_i[:], [[1, 1]], base=0, channel_multiplier=1).then_inc(s_iota, 1)
                pool.wait_ge(s_wmax, 1)
                nc.gpsimd.partition_all_reduce(wabs[:], wmax[:], P, bass.bass_isa.ReduceOp.absmax
                                               ).then_inc(s_wabs, 1)
                nc.gpsimd.memset(pad_p[:], 0.0)
                nc.gpsimd.memset(fill[:, :, 0:2], 0)
                nc.gpsimd.memset(fill[:, :, 2:3].bitcast(F32), -1.0).then_inc(s_fill0, 1)
                pool.wait_ge(s_most, 1)
                with pool.If(pool.value_load(most[0:1, 0:1], min_val=0, max_val=E) > WIN):
                    rows_v = list_dram.rearrange("(c p r) k -> c p (r k)", p=P, r=TILES)
                    pool.wait_ge(s_fill0, 1)
                    with pool.Fori(0, TILES * SLOTS // (P * TILES)) as c:
                        pool.dma_start(rows_v[bass.ds(c, 1), :, :].rearrange("o p k -> (o p) k"),
                                       fill[:].rearrange("p r k -> p (r k)")).then_inc(s_fill, 16)
                        pool.wait_ge(s_fill, c * 16 + 16)
                    with pool.Fori(0, EC) as c:
                        nc.gpsimd.tensor_copy(pos_c[:], pos_i[:, bass.ds(c, 1)])
                        nc.gpsimd.tensor_copy(row_c[:], row_i[:, bass.ds(c, 1), :].rearrange("p o k -> p (o k)")
                                              ).then_inc(s_col, 1)
                        pool.wait_ge(s_col, c + 1)
                        nc.gpsimd.tensor_tensor(pad_p[:], pad_p[:], pad_p[:], ALU.add)
                        nc.gpsimd.indirect_dma_start(list_dram, bass.IndirectOffsetOnAxis(pos_c[:, 0:1], 0),
                                                     row_c[:], None).then_inc(s_scatter, 16)
                        pool.wait_ge(s_scatter, c * 16 + 16)

            @block.scalar
            def _(act):
                act.wait_ge(s_wscale, 1)
                for i in range(3):
                    nc.scalar.activation(w_hi[i][:], stage[i][:], ACT.Copy, scale=wscale[:, i:i + 1]
                                         ).then_inc(s_whi, 1)

            @block.tensor
            def _(pe):
                pe.wait_ge(s_oh, 1)
                for c in range(EC):
                    last = nc.tensor.matmul(ps_t[0:M, 0, 0:TILES], oh_b[:, c, :], oh_a[:, c, :],
                                            start=(c == 0), stop=(c == EC - 1))
                last.then_inc(s_count, 1)
                pe.wait_ge(s_cum, 1)
                for k in range(RBATCH):
                    if k >= 2:
                        pe.wait_ge(s_rank_used, k - 1)
                    for c in range(k * RB, min(EC, (k + 1) * RB)):
                        o = ps_u[k % 2][0:EP, (c - k * RB) * TILES:(c - k * RB + 1) * TILES]
                        nc.tensor.matmul(o, before[:], oh_a[:, c, :], start=True, stop=False)
                        last = nc.tensor.matmul(o, ones16[:], cum[:, c, :], start=False, stop=True)
                    last.then_inc(s_rank_mm, 1)
                last = nc.tensor.matmul(ps_t[0:EP, 1, 0:TILES], ones16[:], cum[:, EC, :], start=True, stop=True)
                last.then_inc(s_total, 1)
                pe.wait_ge(s_vals, 1)
                for c in range(EC):
                    last = nc.tensor.matmul(ps_y[:, 0, 0:3 * TILES], oh_r[:, c, :],
                                            vals[:, c, :, :].rearrange("p k t -> p (k t)"),
                                            start=(c == 0), stop=(c == EC - 1))
                last.then_inc(s_lists, 1)

            @block.vector
            def _(dve):
                n = [0]

                def link(ins):
                    n[0] += 1
                    ins.then_inc(s_chain, 1)
                    dve.wait_ge(s_chain, n[0])

                V = nc.vector
                dve.wait_ge(s_iota, 1)
                V.tensor_copy(iota_row[:], iota_row_i[:])
                link(V.tensor_copy(iota_part[:], iota_part_i[:]))
                V.memset(ones16[:], 1.0)
                V.memset(cum[:, 0, :], 0.0)
                V.tensor_scalar(ident16[:], iota_row[:], iota_part[:], None, ALU.is_equal)
                V.tensor_scalar(ident[:], iota_row[:], iota_part[:], None, ALU.is_equal)
                V.tensor_scalar(rank8[:], iota_row[:, 0:NE], -1.0, float(NE), ALU.mult, ALU.add)
                V.tensor_scalar(before[:], iota_row[0:EP, 0:EP], iota_part[0:EP, :], None, ALU.is_gt)
                dve.wait_ge(s_edges, 32)
                V.tensor_copy(src_f, src_i[:])
                link(V.tensor_copy(dst_f, dst_i[:]))
                V.tensor_scalar(q_i[:, 0, :], dst_f, 0.5, 1.0 / TILES, ALU.add, ALU.mult)
                link(V.tensor_scalar(q_i[:, 1, :], src_f, 0.5, 1.0 / SRC_LO, ALU.add, ALU.mult))
                V.tensor_copy(q_f, q_i[:, 0, :])
                link(V.tensor_copy(hi_f, q_i[:, 1, :]))
                V.scalar_tensor_tensor(lo_f, hi_f, -float(SRC_LO), src_f, ALU.mult, ALU.add)
                link(V.scalar_tensor_tensor(r_f, q_f, -float(TILES), dst_f, ALU.mult, ALU.add))
                link(V.tensor_scalar(neg_f, r_f, 0.0, None, ALU.is_lt))
                V.scalar_tensor_tensor(a_f, neg_f, float(TILES), r_f, ALU.mult, ALU.add)
                link(V.tensor_tensor(b1_f, q_f, neg_f, ALU.subtract))
                V.tensor_tensor(oh_a[:], a_f.unsqueeze(2).to_broadcast([EP, EC, TILES]),
                                iota_row[0:EP, 0:TILES].unsqueeze(1).to_broadcast([EP, EC, TILES]),
                                ALU.is_equal)
                link(V.tensor_tensor(oh_b[:], b1_f.unsqueeze(2).to_broadcast([EP, EC, M]),
                                     iota_row[0:EP, 0:M].unsqueeze(1).to_broadcast([EP, EC, M]),
                                     ALU.is_equal))
                V.engine_nop().then_inc(s_oh, 1)
                link(V.tensor_scalar(b1_f, b1_f, 1.0, None, ALU.add))
                for c in range(EC):
                    link(V.tensor_tensor(cum[:, c + 1, :], cum[:, c, :], oh_a[:, c, :], ALU.add))
                V.engine_nop().then_inc(s_cum, 1)
                for k, v in enumerate((hi_f, lo_f, b1_f)):
                    V.tensor_tensor(vals[:, :, k, :], oh_a[:], v.unsqueeze(2).to_broadcast([EP, EC, TILES]),
                                    ALU.mult)
                for k in range(RBATCH):
                    dve.wait_ge(s_rank_mm, k + 1)
                    c0, c1 = k * RB, min(EC, (k + 1) * RB)
                    w = c1 - c0
                    link(V.tensor_tensor(picked[:, 0:w, :], oh_a[:, c0:c1, :],
                                         ps_u[k % 2][0:EP, 0:w * TILES].rearrange("p (c t) -> p c t", c=w),
                                         ALU.mult))
                    V.engine_nop().then_inc(s_rank_used, 1)
                    link(V.tensor_reduce(rank_f[:, c0:c1], picked[:, 0:w, :], AX.X, ALU.add))
                V.tensor_tensor(oh_r[:], rank_f.unsqueeze(2).to_broadcast([EP, EC, WIN]),
                                iota_row[0:EP, 0:WIN].unsqueeze(1).to_broadcast([EP, EC, WIN]),
                                ALU.is_equal).then_inc(s_vals, 1)
                dve.wait_ge(s_total, 1)
                V.tensor_reduce(most[:], ps_t[0:1, 1, 0:TILES], AX.X, ALU.max)
                V.tensor_copy(row_i[:, :, 0], src_f)
                V.tensor_copy(row_i[:, :, 1], dst_f)
                V.tensor_scalar(row_i[:, :, 2].bitcast(F32), b1_f, -1.0, None, ALU.add)
                V.scalar_tensor_tensor(pos_i[:], a_f, float(SLOTS), rank_f, ALU.mult, ALU.add).then_inc(s_most, 1)
                dve.wait_ge(s_count, 1)
                deg, half, y, u = tmp_w[0:M, 0, :], newton[0:M, 1, :], newton[0:M, 0, :], newton[0:M, 2, :]
                link(V.tensor_scalar(deg, ps_t[0:M, 0, 0:TILES], 1.0, None, ALU.add))
                V.tensor_scalar(half, deg, -0.5, None, ALU.mult)
                link(V.tensor_scalar(y.bitcast(I32), deg.bitcast(I32), -0.5, float(RSQRT_MAGIC),
                                     ALU.mult, ALU.add))
                for _i in range(4):
                    link(V.tensor_tensor(u, y, y, ALU.mult))
                    link(V.tensor_tensor(u, u, half, ALU.mult))
                    link(V.scalar_tensor_tensor(y, u, 1.5, y, ALU.add, ALU.mult))
                V.engine_nop().then_inc(s_dinv, 1)
                link(V.reciprocal(deg_inv[0:M, :], deg))
                link(V.tensor_scalar(deg_inv[0:M, :], deg_inv[0:M, :], XS, None, ALU.mult))
                for i in range(3):
                    dve.wait_ge(s_w[i], 16)
                    V.tensor_reduce(wmax[:, i:i + 1], stage[i][:], AX.XY, ALU.max, apply_absolute_value=True)
                dve.wait_ge(s_w[3], 16)
                V.tensor_reduce(wmax[:, 3:4], gate_f[:], AX.XY, ALU.max, apply_absolute_value=True
                                ).then_inc(s_wmax, 1)
                dve.wait_ge(s_wabs, 1)
                link(V.tensor_scalar(wabs[:], wabs[:], 2.0 ** -100, None, ALU.max))
                link(V.tensor_scalar(wexp[:], wabs[:].bitcast(I32), 0x7F800000, None, ALU.bitwise_and))
                B23 = float(2 ** 23)
                V.tensor_scalar(wscale[:].bitcast(I32), wexp[:], -1.0, (254 + W_LOG) * B23, ALU.mult, ALU.add)
                V.tensor_scalar(v_scale.bitcast(I32), wexp[:, 1:2], -1.0, (254 + 4) * B23, ALU.mult, ALU.add)
                V.tensor_scalar(wun[:].bitcast(I32), wexp[:], -(W_LOG + XS_LOG) * B23, None, ALU.add)
                V.tensor_scalar(scales[:, 5:6].bitcast(I32), wexp[:, 2:3], -W_LOG * B23, None, ALU.add)
                link(V.tensor_scalar(scales[:, 6:7].bitcast(I32), wexp[:, 1:2], -4 * B23, None, ALU.add))
                V.engine_nop().then_inc(s_wscale, 1)
                V.tensor_copy(scales[:, 0:2], wun[:, 0:2])
                V.tensor_copy(inv_gate, wun[:, 3:4])
                V.tensor_tensor(inv_out, scales[:, 5:6], scales[:, 6:7], ALU.mult)
                link(V.tensor_scalar(gate[:, :, 0:NE], gate_f[:], wscale[:, 3:4], None, ALU.mult))
                V.scalar_tensor_tensor(gate[:, :, NE:2 * NE], gate_f[:], wscale[:, 3:4], gate[:, :, 0:NE],
                                       ALU.mult, ALU.subtract)
                dve.wait_ge(s_lists, 1)
                link(V.tensor_copy(lists[:], ps_y[:, 0, 0:3 * TILES].rearrange("p (k t) -> p k t", k=3)))
                V.scalar_tensor_tensor(win_src[:], lists[:, 0, :], float(SRC_LO), lists[:, 1, :],
                                       ALU.mult, ALU.add)
                V.tensor_scalar(win_b[:], lists[:, 2, :], -1.0, None, ALU.add)
                link(V.tensor_scalar(tmp_w[:, 1, :], lists[:, 2, :], -1.0, 0.0, ALU.add, ALU.max))
                V.scalar_tensor_tensor(win_dst[:], tmp_w[:, 1, :], float(TILES), iota_row[:, 0:TILES],
                                       ALU.mult, ALU.add)
                for i in range(3):
                    dve.wait_ge(s_whi, i + 1)
                    last = V.scalar_tensor_tensor(w_lo[i][:].rearrange("p c n -> p (c n)"),
                                                  stage[i][:].rearrange("p c n -> p (c n)"),
                                                  wscale[:, i:i + 1],
                                                  w_hi[i][:].rearrange("p c n -> p (c n)"),
                                                  ALU.mult, ALU.subtract)
                link(last)
        prep.close()

        x_in = sb("x_in", [M, GT, D], F32)
        x_e = sb("x_e", [P, GT, D], F32)
        dsd = sb("dsd", [P, GT, 2], F32)
        z = sb("z", [M, D], F32)
        z_hi = sb("z_hi", [M, 2, D], F16)
        z_lo = sb("z_lo", [M, 2, D], F16)
        ze = sb("ze", [P, D], F32)
        ze_hi = sb("ze_hi", [P, 2, D], F16)
        ze_lo = sb("ze_lo", [P, 2, D], F16)
        hit = sb("hit", [P, 2, M], F16)
        a_hi = sb("a_hi", [P, KC, P], F16)
        a_lo = sb("a_lo", [P, KC, P], F16)
        x1 = sb("x1", [M, 2 * GT, D], F32)
        x2 = sb("x2", [M, D], F32)
        xt_hi = sb("xt_hi", [P, KC, GT, P], F16)
        xt_lo = sb("xt_lo", [P, KC, GT, P], F16)
        u_act = sb("u_act", [P, 2, GT * M], F32)
        v_f = sb("v_f", [P, 2, GT * M], F32)
        v_hi = sb("v_hi", [P, KC, GT, P], F16)
        v_lo = sb("v_lo", [P, KC, GT, P], F16)
        gates_t = sb("gates_t", [P, GT * M], F32)
        gates_rep = sb("gates_rep", [M, GT, P], F32)
        o_st = sb("o_st", [M, 2, D], F32)
        st = sb("st", [P, 2, GT, 2, 6], F32)
        mv = sb("mv", [P, 2, GT, 2], F32)
        nt = sb("nt", [P, 5, 2, GT], F32)
        st2 = sb("st2", [M, 2, 6], F32)
        mv2 = sb("mv2", [M, 2], F32)
        nt2 = sb("nt2", [M, 6], F32)
        pad = sb("pad", [1, P], F32)
        lg = sb("lg", [M, GT, 32], F32)
        rt = sb("rt", [M, 7, GT, NE], F32)
        r1 = sb("r1", [M, 6, GT], F32)
        ov_list = sb("ov_list", [P, 3], I32)
        ov_x = sb("ov_x", [P, D], F32)
        ov_dsd = sb("ov_dsd", [P, 2], F32)
        ov_st = sb("ov_st", [P, 2, 6], F32)
        ov_mv = sb("ov_mv", [P, 2], F32)
        ov_nt = sb("ov_nt", [P, 6], F32)
        ov_z = sb("ov_z", [P, D], F32)
        ov_hi = sb("ov_hi", [P, D], F16)
        ov_lo = sb("ov_lo", [P, D], F16)
        ov_hit = sb("ov_hit", [P, M], F16)
        ov_sum = sb("ov_sum", [M, D], F32)
        idx_cols = sb("idx_cols", [P, GT, 2], I32)
        half1, y1_, u1, sc1, bi1 = (nt[:, i, :, :] for i in range(5))

        s_x = [sem(f"s_xin{t}") for t in range(GT)]
        s_xe = [sem(f"s_xe{t}") for t in range(GT)]
        s_ln1 = sem("s_ln1")
        s_z = sem("s_z")
        s_zlo = sem("s_zlo")
        s_xb = sem("s_xb")
        s_t1 = sem("s_t1")
        s_ahi = sem("s_ahi")
        s_alo = sem("s_alo")
        s_y = sem("s_y")
        s_x1 = sem("s_x1")
        s_ln2 = sem("s_ln2")
        s_x2 = sem("s_x2")
        s_t2 = sem("s_t2")
        s_xthi = sem("s_xthi")
        s_xtlo = sem("s_xtlo")
        s_r = sem("s_r")
        s_lmax = sem("s_lmax")
        s_exp = sem("s_exp")
        s_gates = sem("s_gates")
        s_gt = sem("s_gt")
        s_gs = sem("s_gs")
        s_u = sem("s_u")
        s_gelu = sem("s_gelu")
        s_v = sem("s_v")
        s_vhi = sem("s_vhi")
        s_vlo = sem("s_vlo")
        s_d = sem("s_d")
        s_o = sem("s_o")
        s_st = [sem(f"s_st{i}") for i in range(2)]
        s_idx = sem("s_idx")
        s_ovl = sem("s_ovl")
        s_ovx = sem("s_ovx")
        s_ovr = sem("s_ovr")
        s_ovm = sem("s_ovm")
        s_ovs = sem("s_ovs")
        s_ovp = sem("s_ovp")
        s_ovlink = sem("s_ovlink")
        s_ovz = sem("s_ovz")
        s_link = sem("s_link")

        def until(eng, sm, value):
            if isinstance(value, int) and value <= 0:
                return
            eng.wait_ge(sm, value)

        def counters(eng):
            done = eng.alloc_register(f"windows_{eng.engine.name}")
            eng.reg_mov(done, 0)
            return eng.value_load(most[0:1, 0:1], min_val=0, max_val=E), done

        def further_windows(eng, full, done, window):
            with eng.Fori(1, ROUNDS) as r:
                with eng.If(full > r * WIN):
                    window(r, eng.snap(done, min_val=0, max_val=TILES * ROUNDS))
                    eng.reg_add(done, done, 1)

        def over_groups(eng, body):
            body(0, True, False)
            with eng.Fori(1, GROUPS - 1) as g:
                body(g, False, False)
            body(GROUPS - 1, False, True)

        def x1_at(g, t):
            return x1[:, bass.ds((g % 2) * GT + t, 1), :].rearrange("p o d -> p (o d)")

        turned = ps_t[:, :, 0:3 * P].rearrange("p b (c n) -> p b c n", c=3)[:, :, :, 0:M]

        def chunks(part):
            return part.rearrange("p (b c) n -> p b c n", b=2)[:, :, :, 0:M]

        with nc.Block() as block:
            @block.sync
            def _(sp):
                for t in range(GT):
                    sp.dma_start(x_in[:, t, :], x_t[:, t, :]).then_inc(s_x[t], 16)

                def store(g, t):
                    until(sp, s_o, g * GT + t + 1)
                    sp.dma_start(out_t[:, bass.ds(g * GT + t, 1), :].rearrange("p o d -> p (o d)"),
                                 o_st[:, t % 2, :]).then_inc(s_st[t % 2], 16)

                def body(g, first, last):
                    for t in range(GT):
                        if not last:
                            until(sp, s_x1, g * GT + t + 1)
                            sp.dma_start(x_in[:, t, :],
                                         x_t[:, bass.ds((g + 1) * GT + t, 1), :].rearrange("p o d -> p (o d)")
                                         ).then_inc(s_x[t], 16)
                        if not first:
                            store(g - 1, t)

                over_groups(sp, body)
                for t in range(GT):
                    store(GROUPS - 1, t)
                for i in range(2):
                    sp.wait_ge(s_st[i], 16 * TILES // 2)

            @block.gpsimd
            def _(pool):
                def gather(g, t):
                    for o, table, side in ((x_e[:, t, :], x, 0), (dsd[:, t, 0:1], dinv_dram, 0),
                                           (dsd[:, t, 1:2], dinv_dram, 1)):
                        nc.gpsimd.indirect_dma_start(o, None, table, bass.IndirectOffsetOnAxis(
                            idx_cols[:, t, side:side + 1], 0)).then_inc(s_xe[t], 16)

                def columns(g):
                    nc.gpsimd.tensor_copy(idx_cols[:, :, 0], win_src[:, bass.ds(g * GT, GT)])
                    nc.gpsimd.tensor_copy(idx_cols[:, :, 1], win_dst[:, bass.ds(g * GT, GT)]).then_inc(s_idx, 1)
                    until(pool, s_idx, g + 1)

                full, done = counters(pool)
                nc.gpsimd.memset(pad_p[:], 0.0).then_inc(s_ovp, 1)

                def further(T):
                    def window(r, k):
                        pool.wait_ge(s_ovp, k + 1)
                        pool.wait_ge(s_ovs, k + 1)
                        pool.dma_start(ov_list[0:WIN, :], list_dram[bass.ds(T * SLOTS + r * WIN, WIN), :]
                                       ).then_inc(s_ovl, 16)
                        pool.wait_ge(s_ovl, k * 16 + 16)
                        nc.gpsimd.tensor_tensor(pad_p[:], bias_row[0:1, 0:1], bias_row[0:1, 0:1], ALU.add
                                                ).then_inc(s_ovp, 1)
                        for o, table, side in ((ov_x[:], x, 0), (ov_dsd[:, 0:1], dinv_dram, 0),
                                               (ov_dsd[:, 1:2], dinv_dram, 1)):
                            nc.gpsimd.indirect_dma_start(o, None, table, bass.IndirectOffsetOnAxis(
                                ov_list[:, side:side + 1], 0)).then_inc(s_ovx, 16)

                    with pool.If(full > WIN):
                        further_windows(pool, full, done, window)

                columns(0)
                for t in range(GT):
                    gather(0, t)
                further(0)

                def body(g, first, last):
                    if not last:
                        for t in range(GT):
                            until(pool, s_xe[t], 48 * (g + 1))
                        columns(g + 1)
                    for t in range(GT):
                        until(pool, s_z, g * GT + t + 1)
                        nc.gpsimd.tensor_tensor(x_in[:, t, :], x_in[:, t, :], bias_row[0:M, :],
                                                ALU.add).then_inc(s_xb, 1)
                        if not last:
                            gather(g + 1, t)
                        if not (last and t == GT - 1):
                            further(g * GT + t + 1)

                over_groups(pool, body)

            @block.scalar
            def _(act):
                A = nc.scalar

                def split_z(g, t):
                    T = g * GT + t
                    until(act, s_ln1, g + 1)
                    until(act, s_t1, T - 1)
                    until(act, s_zlo, T)
                    for part in (z[:], z_hi[:, t % 2, :]):
                        A.activation(part, x_in[:, t, :], ACT.Identity, bias=bi1[0:M, 0, t:t + 1],
                                     scale=sc1[0:M, 0, t:t + 1])
                    A.activation(ze[:], x_e[:, t, :], ACT.Identity, bias=bi1[:, 1, t:t + 1],
                                 scale=sc1[:, 1, t:t + 1])
                    A.activation(ze_hi[:, t % 2, :], x_e[:, t, :], ACT.Identity, bias=bi1[:, 1, t:t + 1],
                                 scale=sc1[:, 1, t:t + 1]).then_inc(s_z, 1)

                def a_high(g, t):
                    T = g * GT + t
                    until(act, s_t1, T + 1)
                    until(act, s_y, T)
                    A.activation(chunks(a_hi[:]), turned, ACT.Copy).then_inc(s_ahi, 1)

                def norm2(g, t):
                    T = g * GT + t
                    until(act, s_ln2, T + 1)
                    until(act, s_t2, T)
                    A.activation(x2[:], x1_at(g, t), ACT.Identity, bias=nt2[:, 5:6], scale=nt2[:, 4:5]
                                 ).then_inc(s_x2, 1)

                def xt_high(g, t):
                    T = g * GT + t
                    until(act, s_t2, T + 1)
                    if t == 0:
                        until(act, s_u, g * KC)
                    A.activation(chunks(xt_hi[:, :, t, :]), turned, ACT.Copy).then_inc(s_xthi, 1)

                def gelu(g, c):
                    k = g * KC + c
                    until(act, s_u, k + 1)
                    until(act, s_v, k - 1)
                    A.activation(u_act[:, c % 2, :], ps_u[(c + 1) % 2][:, 0:GT * M], ACT.Gelu_apprx_tanh,
                                 scale=inv_fc).then_inc(s_gelu, 1)

                def v_high(g, c):
                    k = g * KC + c
                    until(act, s_v, k + 1)
                    if c == 0:
                        until(act, s_d, g * GT)
                    A.activation(v_hi[:, c, :, 0:M], v_f[:, c % 2, :].rearrange("p (t n) -> p t n", t=GT),
                                 ACT.Copy).then_inc(s_vhi, 1)

                split_z(0, 0)
                split_z(0, 1)
                a_high(0, 0)

                def body(g, first, last):
                    for t in range(GT):
                        if t < GT - 1:
                            a_high(g, t + 1)
                        if t < GT - 2:
                            split_z(g, t + 2)
                        if t > 0:
                            xt_high(g, t - 1)
                        norm2(g, t)
                    xt_high(g, GT - 1)
                    if not last:
                        split_z(g + 1, 0)
                    until(act, s_lmax, g + 1)
                    A.activation(rt[:, 1, :, :], rt[:, 0, :, :], ACT.Exp).then_inc(s_exp, 1)
                    gelu(g, 0)
                    gelu(g, 1)
                    until(act, s_gt, g + 1)
                    A.activation(gates_t[:].rearrange("p (t n) -> p t n", t=GT),
                                 ps_y[:, 0, :].rearrange("p (t n) -> p t n", t=GT)[:, :, 0:M],
                                 ACT.Copy).then_inc(s_gs, 1)
                    v_high(g, 0)
                    gelu(g, 2)
                    v_high(g, 1)
                    if not last:
                        split_z(g + 1, 1)
                    gelu(g, 3)
                    v_high(g, 2)
                    gelu(g, 4)
                    v_high(g, 3)
                    if not last:
                        a_high(g + 1, 0)
                    gelu(g, 5)
                    v_high(g, 4)
                    v_high(g, 5)

                over_groups(act, body)

            @block.tensor
            def _(pe):
                MM = nc.tensor.matmul
                full, done = counters(pe)

                def window(r, k):
                    pe.wait_ge(s_ovr, k + 1)
                    for h in range(2):
                        cols = slice(h * HALF, (h + 1) * HALF)
                        MM(ps_t[0:M, h, 0:HALF], ov_hit[:], ov_hi[:, cols], start=True, stop=False)
                        last = MM(ps_t[0:M, h, 0:HALF], ov_hit[:], ov_lo[:, cols], start=False, stop=True)
                    last.then_inc(s_ovm, 1)
                    pe.wait_ge(s_ovs, k + 2)

                def further():
                    with pe.If(full > WIN):
                        further_windows(pe, full, done, window)

                def aggregate(g, t):
                    T = g * GT + t
                    until(pe, s_alo, T)
                    until(pe, s_xtlo, prior_t2(g, t))
                    if t >= 2:
                        further()
                    until(pe, s_zlo, T + 1)
                    for c in range(KC):
                        o = ps_t[:, c // 3, (c % 3) * P:(c % 3) * P + M]
                        k = slice(c * P, (c + 1) * P)
                        MM(o, z_hi[:, t % 2, k], ident16[0:M, 0:M], start=True, stop=False)
                        MM(o, z_lo[:, t % 2, k], ident16[0:M, 0:M], start=False, stop=False)
                        MM(o, ze_hi[:, t % 2, k], hit[:, t % 2, :], start=False, stop=False)
                        last = MM(o, ze_lo[:, t % 2, k], hit[:, t % 2, :], start=False, stop=True)
                    last.then_inc(s_t1, 1)

                def prior_t2(g, t):
                    return g * GT + max(t - 2, 0)

                def rows(ps, hi, lo, w, c0=0, c1=KC):
                    for c in range(c0, c1):
                        for part, wt in ((hi, w_hi[w]), (hi, w_lo[w]), (lo, w_hi[w])):
                            for h in range(2):
                                last = MM(ps[:, h, 0:HALF], part[:, c, :], wt[:, c, h * HALF:(h + 1) * HALF],
                                          start=(c == 0 and part is hi and wt is w_hi[w]),
                                          stop=(c == KC - 1 and part is lo))
                    return last

                def gnn(g, t):
                    T = g * GT + t
                    until(pe, s_alo, T + 1)
                    until(pe, s_x1, T)
                    if t == 0:
                        until(pe, s_gs, g)
                    rows(ps_y, a_hi, a_lo, 0).then_inc(s_y, 1)

                def down(g, t, c0=0, c1=KC):
                    T = g * GT + t
                    if t == 0:
                        until(pe, s_vlo, (g + 1) * KC)
                    if c0 == 0:
                        until(pe, s_o, T)
                    last = rows(ps_d, v_hi[:, :, t, :], v_lo[:, :, t, :], 2, c0, c1)
                    if c1 == KC:
                        last.then_inc(s_d, 1)

                def turn(g, t):
                    T = g * GT + t
                    until(pe, s_x2, T + 1)
                    until(pe, s_alo, g * GT + min(t + 3, GT))
                    until(pe, s_xtlo, T)
                    for c in range(KC):
                        last = nc.tensor.transpose(ps_t[:, c // 3, (c % 3) * P:(c % 3) * P + M],
                                                   x2[:, c * P:(c + 1) * P], ident[0:M, 0:M])
                    last.then_inc(s_t2, 1)

                def router(g, t):
                    until(pe, s_xthi, g * GT + t + 1)
                    if t == 0:
                        until(pe, s_gelu, g * KC)
                    for c in range(KC):
                        MM(ps_u[0][:, t * 32:t * 32 + 2 * NE], xt_hi[:, c, t, :], gate[:, c, :],
                           start=(c == 0), stop=(c == KC - 1))
                    if t < GT - 1:
                        router_low(g, t)

                def router_low(g, t):
                    until(pe, s_xtlo, g * GT + t + 1)
                    for c in range(KC):
                        last = MM(ps_u[0][:, t * 32 + 2 * NE:t * 32 + 3 * NE], xt_lo[:, c, t, :],
                                  gate[:, c, 0:NE], start=(c == 0), stop=(c == KC - 1))
                    if t == GT - 1:
                        last.then_inc(s_r, 1)

                def up(g, m):
                    k = g * KC + m
                    if m == 0:
                        until(pe, s_gelu, k - 1)
                    elif m == 1:
                        until(pe, s_lmax, g + 1)
                    else:
                        until(pe, s_gelu, k - 1)
                    o = ps_u[(m + 1) % 2][:, 0:GT * M]
                    n = slice(m * P, (m + 1) * P)
                    if m == 0:
                        for c in range(KC):
                            MM(o, w_hi[1][:, c, n], xt_hi[:, c, :, 0:M], start=(c == 0), stop=False)
                            MM(o, w_lo[1][:, c, n], xt_hi[:, c, :, 0:M], start=False, stop=False)
                        router_low(g, GT - 1)
                        for c in range(KC):
                            last = MM(o, w_hi[1][:, c, n], xt_lo[:, c, :, 0:M], start=False, stop=(c == KC - 1))
                    else:
                        for c in range(KC):
                            MM(o, w_hi[1][:, c, n], xt_hi[:, c, :, 0:M], start=(c == 0), stop=False)
                            MM(o, w_hi[1][:, c, n], xt_lo[:, c, :, 0:M], start=False, stop=False)
                            last = MM(o, w_lo[1][:, c, n], xt_hi[:, c, :, 0:M], start=False, stop=(c == KC - 1))
                    last.then_inc(s_u, 1)

                def turn_gates(g):
                    until(pe, s_gates, g + 1)
                    until(pe, s_x1, (g + 1) * GT)
                    for t in range(GT):
                        last = nc.tensor.transpose(ps_y[:, 0, t * P:t * P + M], gates_rep[:, t, :],
                                                   ident[0:M, 0:M])
                    last.then_inc(s_gt, 1)

                further()
                further()
                aggregate(0, 0)

                def body(g, first, last):
                    for t in range(GT - 1):
                        gnn(g, t)
                        aggregate(g, t + 1)
                        if not first:
                            down(g - 1, t)
                        if t > 0:
                            turn(g, t - 1)
                    gnn(g, 3)
                    router(g, 0)
                    router(g, 1)
                    turn(g, 2)
                    if not first:
                        down(g - 1, 3, 0, KC - 1)
                    router(g, 2)
                    turn(g, 3)
                    if not first:
                        down(g - 1, 3, KC - 1, KC)
                    router(g, 3)
                    up(g, 0)
                    if not last:
                        further()
                    up(g, 1)
                    up(g, 2)
                    turn_gates(g)
                    up(g, 3)
                    if not last:
                        further()
                    up(g, 4)
                    if not last:
                        aggregate(g + 1, 0)
                    up(g, 5)

                over_groups(pe, body)
                for t in range(GT):
                    down(GROUPS - 1, t)

            @block.vector
            def _(dve):
                V = nc.vector
                n, pads = [0, 0], []

                def link(ins):
                    n[1] += 1
                    ins.then_inc(s_link, 1)
                    dve.wait_ge(s_link, n[0] + n[1])

                def stats1(g, t):
                    until(dve, s_x[t], 16 * (g + 1))
                    until(dve, s_xe[t], 48 * (g + 1))
                    for h in range(2):
                        V.bn_stats(st[0:M, 0, t, h, :], x_in[:, t, h * HALF:(h + 1) * HALF])
                        last = V.bn_stats(st[:, 1, t, h, :], x_e[:, t, h * HALF:(h + 1) * HALF])
                    return last

                def carry_wait():
                    pads.append(0)
                    V.memset(pad[:, len(pads) - 1:len(pads)], 0.0)

                def rsqrt(y, half, u, var, link):
                    V.tensor_scalar(half, var, EPS, -0.5, ALU.add, ALU.mult)
                    link(V.tensor_scalar(u, var, EPS, None, ALU.add))
                    link(V.tensor_scalar(y.bitcast(I32), u.bitcast(I32), -0.5, float(RSQRT_MAGIC),
                                         ALU.mult, ALU.add))
                    for _i in range(3):
                        if y.free_size() == 1:
                            link(V.scalar_tensor_tensor(u, y, half, y, ALU.mult, ALU.mult))
                        else:
                            link(V.tensor_tensor(u, y, y, ALU.mult))
                            link(V.tensor_tensor(u, u, half, ALU.mult))
                        link(V.scalar_tensor_tensor(y, u, 1.5, y, ALU.add, ALU.mult))

                def finish1(g):
                    carry_wait()
                    for t in range(GT):
                        V.bn_aggr(mv[0:M, 0, t, :], st[0:M, 0, t, :, :].rearrange("p a b -> p (a b)"))
                        last = V.bn_aggr(mv[:, 1, t, :], st[:, 1, t, :, :].rearrange("p a b -> p (a b)"))
                    link(last)
                    rsqrt(y1_, half1, u1, mv[:, :, :, 1], link)
                    until(dve, s_z, g * GT)
                    V.tensor_tensor(sc1[0:M, 0, :], y1_[0:M, 0, :], deg_inv[0:M, bass.ds(g * GT, GT)], ALU.mult)
                    link(V.tensor_tensor(u1[:, 1, :], dsd[:, :, 0], dsd[:, :, 1], ALU.mult))
                    link(V.scalar_tensor_tensor(sc1[:, 1, :], u1[:, 1, :], XS, y1_[:, 1, :], ALU.mult, ALU.mult))
                    V.scalar_tensor_tensor(bi1, mv[:, :, :, 0], -1.0, sc1, ALU.mult, ALU.mult
                                           ).then_inc(s_ln1, 1)

                def window(r, k):
                    steps = [0]

                    def step(ins):
                        steps[0] += 1
                        ins.then_inc(s_ovlink, 1)
                        dve.wait_ge(s_ovlink, k * OV_STEPS + steps[0])

                    dve.wait_ge(s_ovx, k * 48 + 48)
                    carry_wait()
                    V.bn_stats(ov_st[:, 0, :], ov_x[:, 0:HALF])
                    step(V.bn_stats(ov_st[:, 1, :], ov_x[:, HALF:D]))
                    carry_wait()
                    step(V.bn_aggr(ov_mv[:], ov_st[:].rearrange("p a b -> p (a b)")))
                    y, half, u, norm, sc, bi = (ov_nt[:, i:i + 1] for i in range(6))
                    rsqrt(y, half, u, ov_mv[:, 1:2], step)
                    step(V.tensor_tensor(norm, ov_dsd[:, 0:1], ov_dsd[:, 1:2], ALU.mult))
                    step(V.scalar_tensor_tensor(sc, norm, XS, y, ALU.mult, ALU.mult))
                    step(V.scalar_tensor_tensor(bi, ov_mv[:, 0:1], -1.0, sc, ALU.mult, ALU.mult))
                    step(V.tensor_scalar(ov_z[:], ov_x[:], sc, bi, ALU.mult, ALU.add))
                    step(V.tensor_copy(ov_hi[:], ov_z[:]))
                    V.tensor_tensor(ov_lo[:], ov_z[:], ov_hi[:], ALU.subtract)
                    V.tensor_scalar(ov_hit[:], iota_row[:, 0:M], ov_list[:, 2:3].bitcast(F32), None, ALU.is_equal
                                    ).then_inc(s_ovr, 1)
                    dve.wait_ge(s_ovm, k + 1)
                    step(V.tensor_tensor(ov_sum[:].rearrange("p (h n) -> p h n", h=2), ps_t[0:M, :, 0:HALF],
                                         ov_sum[:].rearrange("p (h n) -> p h n", h=2), ALU.add))
                    V.memset(pad[:, P - 1:P], 0.0).then_inc(s_ovs, 1)
                    assert steps[0] == OV_STEPS, steps

                def further(T, t):
                    carry_wait()
                    with dve.If(full > WIN):
                        V.memset(ov_sum[:], 0.0).then_inc(s_ovz, 1)
                        dve.wait_ge(s_ovz, T * 3 + 1)
                        carry_wait()
                        further_windows(dve, full, done, window)
                        V.tensor_tensor(z[:], z[:], ov_sum[:], ALU.add).then_inc(s_ovz, 1)
                        dve.wait_ge(s_ovz, T * 3 + 2)
                        V.tensor_copy(z_hi[:, t % 2, :], z[:]).then_inc(s_ovz, 1)
                        dve.wait_ge(s_ovz, T * 3 + 3)
                        carry_wait()

                def low_z(g, t):
                    T = g * GT + t
                    until(dve, s_z, T + 1)
                    until(dve, s_t1, T - 1)
                    further(T, t)
                    V.tensor_tensor(z_lo[:, t % 2, :], z[:], z_hi[:, t % 2, :], ALU.subtract)
                    V.tensor_tensor(ze_lo[:, t % 2, :], ze[:], ze_hi[:, t % 2, :], ALU.subtract)
                    V.tensor_scalar(hit[:, t % 2, :], iota_row[:, 0:M], win_b[:, bass.ds(T, 1)], None, ALU.is_equal
                                    ).then_inc(s_zlo, 1)

                def a_low(g, t):
                    T = g * GT + t
                    until(dve, s_ahi, T + 1)
                    until(dve, s_y, T)
                    V.tensor_tensor(chunks(a_lo[:]), turned, chunks(a_hi[:]), ALU.subtract).then_inc(s_alo, 1)

                def residual1(g, t):
                    T = g * GT + t
                    until(dve, s_y, T + 1)
                    until(dve, s_xb, T + 1)
                    until(dve, s_x2, T - GT + 1)
                    V.scalar_tensor_tensor(x1_at(g, t).rearrange("p (h n) -> p h n", h=2), ps_y[0:M, :, 0:HALF],
                                           inv_gnn[0:M, :],
                                           x_in[:, t, :].rearrange("p (h n) -> p h n", h=2), ALU.mult, ALU.add
                                           ).then_inc(s_x1, 1)
                    until(dve, s_x1, T + 1)

                def stats2(g, t):
                    T = g * GT + t
                    carry_wait()
                    V.bn_stats(st2[:, 0, :], x1_at(g, t)[:, 0:HALF])
                    link(V.bn_stats(st2[:, 1, :], x1_at(g, t)[:, HALF:D]))
                    carry_wait()
                    link(V.bn_aggr(mv2[:], st2[:].rearrange("p a b -> p (a b)")))
                    var, y, half, u = mv2[:, 1:2], nt2[:, 0:1], nt2[:, 1:2], nt2[:, 2:3]
                    rsqrt(y, half, u, var, link)
                    until(dve, s_x2, T)
                    link(V.tensor_scalar(nt2[:, 4:5], y, XS, None, ALU.mult))
                    V.scalar_tensor_tensor(nt2[:, 5:6], mv2[:, 0:1], -1.0, nt2[:, 4:5], ALU.mult, ALU.mult
                                           ).then_inc(s_ln2, 1)

                def xt_low(g, t):
                    T = g * GT + t
                    until(dve, s_xthi, T + 1)
                    V.tensor_tensor(chunks(xt_lo[:, :, t, :]), turned, chunks(xt_hi[:, :, t, :]), ALU.subtract
                                    ).then_inc(s_xtlo, 1)

                def output(g, t):
                    T = g * GT + t
                    until(dve, s_d, T + 1)
                    until(dve, s_st[t % 2], (g * (GT // 2) + t // 2) * 16)
                    V.scalar_tensor_tensor(o_st[:, t % 2, :].rearrange("p (h n) -> p h n", h=2),
                                           ps_d[0:M, :, 0:HALF], inv_out[0:M, :],
                                           x1_at(g, t).rearrange("p (h n) -> p h n", h=2), ALU.mult, ALU.add
                                           ).then_inc(s_o, 1)

                def logits(g):
                    until(dve, s_r, g + 1)
                    until(dve, s_exp, g)
                    link(V.tensor_scalar(lg[:, :, 0:3 * NE],
                                         ps_u[0][0:M, 0:GT * 32].rearrange("p (t n) -> p t n", t=GT)[:, :, 0:3 * NE],
                                         inv_gate[0:M, :], None, ALU.mult))
                    link(V.tensor_tensor(lg[:, :, 0:NE], lg[:, :, 0:NE], lg[:, :, NE:2 * NE], ALU.add))
                    link(V.tensor_tensor(lg[:, :, 0:NE], lg[:, :, 0:NE], lg[:, :, 2 * NE:3 * NE], ALU.add))
                    link(V.tensor_reduce(r1[:, 0, :], lg[:, :, 0:NE], AX.X, ALU.max))
                    V.tensor_tensor(rt[:, 0, :, :], lg[:, :, 0:NE],
                                    r1[:, 0, :].unsqueeze(2).to_broadcast([M, GT, NE]), ALU.subtract
                                    ).then_inc(s_lmax, 1)
                    until(dve, s_lmax, g + 1)

                def top2(g):
                    L, EX, K, S1, L2, S2, G = (rt[:, i, :, :] for i in range(7))

                    def wide(v):
                        return v.unsqueeze(2).to_broadcast([M, GT, NE])

                    r8 = rank8[0:M, :].unsqueeze(1).to_broadcast([M, GT, NE])
                    link(V.scalar_tensor_tensor(K, L, 0.0, r8, ALU.is_equal, ALU.mult))
                    link(V.tensor_reduce(r1[:, 1, :], K, AX.X, ALU.max))
                    link(V.tensor_tensor(S1, K, wide(r1[:, 1, :]), ALU.is_equal))
                    link(V.scalar_tensor_tensor(L2, S1, -3.0e38, L, ALU.mult, ALU.add))
                    link(V.tensor_reduce(r1[:, 2, :], L2, AX.X, ALU.max))
                    link(V.tensor_tensor(K, L2, wide(r1[:, 2, :]), ALU.is_equal))
                    link(V.tensor_tensor(K, K, r8, ALU.mult))
                    link(V.tensor_reduce(r1[:, 3, :], K, AX.X, ALU.max))
                    link(V.tensor_tensor(S2, K, wide(r1[:, 3, :]), ALU.is_equal))
                    link(V.tensor_tensor(S1, S1, S2, ALU.add))
                    until(dve, s_exp, g + 1)
                    link(V.tensor_tensor(G, EX, S1, ALU.mult))
                    link(V.tensor_reduce(r1[:, 4, :], G, AX.X, ALU.add))
                    link(V.reciprocal(r1[:, 5, :], r1[:, 4, :]))
                    link(V.tensor_tensor(G, G, wide(r1[:, 5, :]), ALU.mult))
                    until(dve, s_gt, g)
                    V.tensor_scalar(gates_rep[:].rearrange("p t (r e) -> p t r e", e=NE),
                                    G.unsqueeze(2).to_broadcast([M, GT, P // NE, NE]),
                                    v_scale[0:M, :], None, ALU.mult).then_inc(s_gates, 1)

                def gated(g, c):
                    k = g * KC + c
                    until(dve, s_gelu, k + 1)
                    if c == 0:
                        until(dve, s_gs, g + 1)
                    until(dve, s_vlo, k - 1)
                    V.tensor_tensor(v_f[:, c % 2, :], u_act[:, c % 2, :], gates_t[:], ALU.mult).then_inc(s_v, 1)

                def low_v(g, c):
                    k = g * KC + c
                    until(dve, s_vhi, k + 1)
                    V.tensor_tensor(v_lo[:, c, :, 0:M], v_f[:, c % 2, :].rearrange("p (t n) -> p t n", t=GT),
                                    v_hi[:, c, :, 0:M], ALU.subtract).then_inc(s_vlo, 1)

                full, done = counters(dve)
                V.memset(mv[:], 1.0)
                V.memset(pad[:, P - 1:P], 0.0).then_inc(s_ovs, 1)
                for part in (a_hi, a_lo, xt_hi, xt_lo, v_hi, v_lo):
                    V.memset(part[:, :, M:P] if len(part.shape) == 3 else part[:, :, :, M:P], 0.0)
                link(V.memset(nt[:], 1.0))
                for t in range(GT):
                    last = stats1(0, t)
                link(last)
                finish1(0)
                low_z(0, 0)
                low_z(0, 1)
                a_low(0, 0)
                n_prologue = n[1]
                counted = []

                def body(g, first, last):
                    n[0], n[1] = n_prologue + g * per_group, 0
                    for t in range(GT):
                        residual1(g, t)
                        if t < GT - 1:
                            a_low(g, t + 1)
                        stats2(g, t)
                        if t < GT - 1 and not first:
                            output(g - 1, t)
                        if t > 0:
                            xt_low(g, t - 1)
                        if t < GT - 2:
                            low_z(g, t + 2)
                        if not last:
                            sums = stats1(g + 1, t)
                    if not last:
                        link(sums)
                        finish1(g + 1)
                    xt_low(g, GT - 1)
                    if not first:
                        output(g - 1, GT - 1)
                    logits(g)
                    top2(g)
                    if not last:
                        low_z(g + 1, 0)
                    gated(g, 0)
                    gated(g, 1)
                    low_v(g, 0)
                    gated(g, 2)
                    low_v(g, 1)
                    if not last:
                        low_z(g + 1, 1)
                    gated(g, 3)
                    low_v(g, 2)
                    gated(g, 4)
                    low_v(g, 3)
                    if not last:
                        a_low(g + 1, 0)
                    gated(g, 5)
                    low_v(g, 4)
                    low_v(g, 5)
                    counted.append(n[1])

                per_group = 77
                over_groups(dve, body)
                assert counted[0] == counted[1] == per_group, counted
                for t in range(GT):
                    output(GROUPS - 1, t)


def _list_rows(nodes, edges, window=128):
    return nodes // 125 * (-(-edges // window) * window)


_INS = ["x", "src", "dst", "L0_gnn_W", "L0_gnn_b", "L0_ffn_w_fc", "L0_ffn_w_proj", "L0_ffn_w_gate"]


def kernel(**inputs):
    import numpy as _np
    import concourse.bacc as _bacc
    from concourse import mybir as _mybir
    from concourse.bass_utils import run_bass_kernel_spmd as _run

    nc = _bacc.Bacc("TRN2", target_bir_lowering=False, num_devices=1)
    arrays, args = {}, []
    for name in _INS:
        a = _np.ascontiguousarray(inputs[name])
        if name == "L0_ffn_w_proj":
            ff, d = a.shape
            ne = inputs["L0_ffn_w_gate"].shape[1]
            a = _np.ascontiguousarray(a.reshape(ff // ne, d, ne).transpose(0, 2, 1).reshape(ff, d))
        arrays[f"in_{name}"] = a
        args.append(nc.dram_tensor(f"in_{name}", a.shape, _mybir.dt.from_np(a.dtype), kind="ExternalInput").ap())
    n, d = inputs["x"].shape
    args.append(nc.dram_tensor("out", (n, d), _mybir.dt.float32, kind="ExternalOutput").ap())
    args.append(nc.dram_tensor("dinv", (n, 1), _mybir.dt.float32, kind="Internal").ap())
    args.append(nc.dram_tensor("edges", (_list_rows(n, inputs["src"].shape[0]), 3), _mybir.dt.int32,
                               kind="Internal").ap())
    gnn_moe_ffn_kernel(nc, *args)
    r = _run(nc, [arrays], core_ids=[0])
    return r.results[0]["out"]
```

```python
import concourse.bass as bass
from concourse import mybir
from contextlib import ExitStack


def gnn_moe_ffn_kernel(nc, x, src, dst, w_gnn, b_gnn, w_fc, w_proj, w_gate, out, dinv_dram, list_dram):
    F32, F16, I32 = mybir.dt.float32, mybir.dt.float16, mybir.dt.int32
    ALU, ACT, AX = mybir.AluOpType, mybir.ActivationFunctionType, mybir.AxisListType

    N, D = x.shape
    E = src.shape[0]
    NE = w_gate.shape[1]
    P = 128
    M = 125
    TILES = N // M
    GT = 4
    GROUPS = TILES // GT
    KC = D // P
    HALF = D // 2
    EP, EC = 125, E // 125
    WIN = P
    ROUNDS = -(-E // WIN)
    SLOTS = ROUNDS * WIN
    SRC_LO = 128
    EPS = 1e-5
    XS_LOG = 4
    XS = float(2 ** XS_LOG)
    W_LOG = 12
    RSQRT_MAGIC = 0x5F3759DF
    OV_STEPS = 16

    x_t = x.rearrange("(p t) d -> p t d", t=TILES)
    out_t = out.rearrange("(p t) d -> p t d", t=TILES)

    ctx = ExitStack()
    with ctx:
        def sb(name, shape, dt, c=ctx):
            return c.enter_context(nc.sbuf_tensor(name, shape, dt))

        def sem(name):
            return ctx.enter_context(nc.semaphore(name))

        w_hi = [sb(f"w_hi_{n}", [P, KC, D], F16) for n in ("gnn", "fc", "proj")]
        w_lo = [sb(f"w_lo_{n}", [P, KC, D], F16) for n in ("gnn", "fc", "proj")]
        gate = sb("gate", [P, KC, 2 * NE], F16)
        ident16 = sb("ident16", [P, P], F16)
        ident = sb("ident", [P, P], F32)
        iota_row = sb("iota_row", [P, P], F32)
        iota_row_i = sb("iota_row_i", [P, P], I32)
        iota_part_i = sb("iota_part_i", [P, 1], I32)
        iota_part = sb("iota_part", [P, 1], F32)
        rank8 = sb("rank8", [P, NE], F32)
        bias_row = sb("bias_row", [P, D], F32)
        scales = sb("scales", [P, 8], F32)
        wmax = sb("wmax", [P, 4], F32)
        wabs = sb("wabs", [P, 4], F32)
        wexp = sb("wexp", [P, 4], I32)
        wscale = sb("wscale", [P, 4], F32)
        wun = sb("wun", [P, 4], F32)
        C_GNN, C_GATE, C_FC, C_PROJ = range(4)
        early = sb("early", [P, 2 * GT * D], F32)
        LATE = KC * GT * P + 5 * GT * M
        late = sb("late", [P, LATE], F32)
        XW = KC * GT * P // 2
        third = sb("third", [P, 2 * XW + 2 * D], F32)
        stage_gnn, stage_proj = third[:, 0:KC * D], late[:, 0:KC * D]
        stage_fc = early[:, 2 * GT * D - KC * D:2 * GT * D]
        gate_f = sb("gate_f", [P, KC, NE], F32)
        v_scale, inv_out, un_fc, un_proj = (scales[:, i:i + 1] for i in range(4))
        inv_gnn, inv_gate, inv_fc = (wun[:, i:i + 1] for i in (C_GNN, C_GATE, C_FC))
        deg_inv = sb("deg_inv", [P, TILES], F32)
        win_src = sb("win_src", [P, TILES], I32)
        win_dst = sb("win_dst", [P, TILES], I32)
        win_b = sb("win_b", [P, TILES], F32)

        pad_p = sb("pad_p", [1, 1], F32)
        most = sb("most", [1, 1], I32)

        ps_t = ctx.enter_context(nc.psum_tensor("ps_t", [P, 2, 512], F32))
        ps_y = ctx.enter_context(nc.psum_tensor("ps_y", [P, 2, 512], F32))
        ps_d = ctx.enter_context(nc.psum_tensor("ps_d", [P, 2, 512], F32))
        ps_u = [ctx.enter_context(nc.psum_tensor(f"ps_u{i}", [P, 512], F32)) for i in range(2)]

        prep = ExitStack()
        src_i = sb("src_i", [EP, EC], I32, prep)
        dst_i = sb("dst_i", [EP, EC], I32, prep)
        q_i = sb("q_i", [EP, 2, EC], I32, prep)
        ed = sb("ed", [EP, 11, EC], F32, prep)
        src_f, dst_f, hi_f, lo_f, q_f, r_f, neg_f, a_f, b_f, b1_f, rank_f = (ed[:, i, :] for i in range(11))
        oh_a = sb("oh_a", [EP, EC, TILES], F16, prep)
        oh_b = sb("oh_b", [EP, EC, M], F16, prep)
        CH = 4
        CL = EC // CH
        assert CH * CL == EC
        cum = sb("cum", [EP, EC, TILES], F16, prep)
        chains = sb("chains", [EP, CH - 1, TILES], F16, prep)
        off_b = sb("off_b", [EP, EC, M], F32, prep)
        before = sb("before", [EP, EP], F16, prep)
        ones16 = sb("ones16", [EP, EP], F16, prep)
        picked = sb("picked", [EP, 6, TILES], F32, prep)
        oh_r = sb("oh_r", [EP, EC, WIN], F16, prep)
        vals = sb("vals", [EP, EC, 3, TILES], F16, prep)
        pos_i = sb("pos_i", [EP, EC], I32, prep)
        row_i = sb("row_i", [EP, EC, 3], I32, prep)
        fill = sb("fill", [P, TILES, 3], I32, prep)
        pos_c = sb("pos_c", [EP, 1], I32, prep)
        row_c = sb("row_c", [EP, 3], I32, prep)
        lists = sb("lists", [P, 3, TILES], F32, prep)
        tmp_w = sb("tmp_w", [P, 2, TILES], F32, prep)
        newton = sb("newton", [P, 3, TILES], F32, prep)

        s_edges = sem("s_edges")
        s_w = [sem(f"s_w{i}") for i in range(4)]
        s_bias = sem("s_bias")
        s_iota = sem("s_iota")
        s_oh = sem("s_oh")
        s_off_b = sem("s_off_b")
        s_oh_a = sem("s_oh_a")
        s_oh_r = sem("s_oh_r")
        s_cum = sem("s_cum")
        s_count = sem("s_count")
        s_rank_mm = sem("s_rank_mm")
        s_rank_used = sem("s_rank_used")
        s_vals = sem("s_vals")
        s_lists = sem("s_lists")
        s_total = sem("s_total")
        s_most = sem("s_most")
        s_fill0 = sem("s_fill0")
        s_fill = sem("s_fill")
        s_col = sem("s_col")
        s_scatter = sem("s_scatter")
        s_dinv = sem("s_dinv")
        s_dinv_st = sem("s_dinv_st")
        s_wmax = sem("s_wmax")
        s_wabs = sem("s_wabs")
        s_wscale = sem("s_wscale")
        s_whi = sem("s_whi")
        s_wlo = sem("s_wlo")
        s_scaled = sem("s_scaled")
        s_wlop = sem("s_wlop")
        s_chain = sem("s_chain")
        RB = 6
        RBATCH = -(-EC // RB)

        def in_chains(h):
            return cum[:, CL - 1, :] if h == 0 else chains[:, h - 1, :]

        def flat(w):
            return w[:].rearrange("p c n -> p (c n)")

        def scale_of(link, c0, c1):
            V, B23 = nc.vector, float(2 ** 23)
            link(V.tensor_scalar(wabs[:, c0:c1], wabs[:, c0:c1], 2.0 ** -100, None, ALU.max))
            link(V.tensor_scalar(wexp[:, c0:c1], wabs[:, c0:c1].bitcast(I32), 0x7F800000, None, ALU.bitwise_and))
            V.tensor_scalar(wscale[:, c0:c1].bitcast(I32), wexp[:, c0:c1], -1.0, (254 + W_LOG) * B23,
                            ALU.mult, ALU.add)
            link(V.tensor_scalar(wun[:, c0:c1].bitcast(I32), wexp[:, c0:c1], -(W_LOG + XS_LOG) * B23, None, ALU.add))

        with nc.Block() as block:
            @block.sync
            def _(sp):
                sp.dma_start(src_i[:], src.rearrange("(p c) -> p c", p=EP)).then_inc(s_edges, 16)
                sp.dma_start(dst_i[:], dst.rearrange("(p c) -> p c", p=EP)).then_inc(s_edges, 16)
                sp.dma_start(gate_f[:], w_gate.rearrange("(c p) n -> p c n", p=P)).then_inc(s_w[C_GATE], 16)
                for i, w, part in ((C_GNN, w_gnn, stage_gnn[:]), (C_FC, w_fc, stage_fc), (C_PROJ, w_proj, stage_proj)):
                    sp.dma_start(part.rearrange("p (c n) -> p c n", c=KC), w.rearrange("(c p) n -> p c n", p=P)
                                 ).then_inc(s_w[i], 16)
                sp.dma_start(bias_row[:], b_gnn.partition_broadcast(P)).then_inc(s_bias, 16)
                sp.wait_ge(s_dinv, 1)
                sp.dma_start(dinv_dram.rearrange("(p t) o -> p (t o)", t=TILES),
                             newton[0:M, 0, :]).then_inc(s_dinv_st, 16)
                sp.wait_ge(s_dinv_st, 16)
                sp.wait_ge(s_bias, 16)

            @block.gpsimd
            def _(pool):
                nc.gpsimd.iota(iota_row_i[:], [[1, P]], base=0, channel_multiplier=0)
                nc.gpsimd.iota(iota_part_i[:], [[1, 1]], base=0, channel_multiplier=1).then_inc(s_iota, 1)
                pool.wait_ge(s_oh_a, 1)
                for k, v in enumerate((hi_f, lo_f, b1_f)):
                    nc.gpsimd.tensor_tensor(vals[:, :, k, :], oh_a[:],
                                            v.unsqueeze(2).to_broadcast([EP, EC, TILES]), ALU.mult
                                            ).then_inc(s_vals, 1)
                nc.gpsimd.memset(pad_p[:], 0.0)
                nc.gpsimd.memset(fill[:, :, 0:2], 0)
                nc.gpsimd.memset(fill[:, :, 2:3].bitcast(F32), -1.0).then_inc(s_fill0, 1)
                pool.wait_ge(s_most, 1)
                with pool.If(pool.value_load(most[0:1, 0:1], min_val=0, max_val=E) > WIN):
                    rows_v = list_dram.rearrange("(c p r) k -> c p (r k)", p=P, r=TILES)
                    pool.wait_ge(s_fill0, 1)
                    with pool.Fori(0, TILES * SLOTS // (P * TILES)) as c:
                        pool.dma_start(rows_v[bass.ds(c, 1), :, :].rearrange("o p k -> (o p) k"),
                                       fill[:].rearrange("p r k -> p (r k)")).then_inc(s_fill, 16)
                        pool.wait_ge(s_fill, c * 16 + 16)
                    with pool.Fori(0, EC) as c:
                        nc.gpsimd.tensor_copy(pos_c[:], pos_i[:, bass.ds(c, 1)])
                        nc.gpsimd.tensor_copy(row_c[:], row_i[:, bass.ds(c, 1), :].rearrange("p o k -> p (o k)")
                                              ).then_inc(s_col, 1)
                        pool.wait_ge(s_col, c + 1)
                        nc.gpsimd.tensor_tensor(pad_p[:], pad_p[:], pad_p[:], ALU.add)
                        nc.gpsimd.indirect_dma_start(list_dram, bass.IndirectOffsetOnAxis(pos_c[:, 0:1], 0),
                                                     row_c[:], None).then_inc(s_scatter, 16)
                        pool.wait_ge(s_scatter, c * 16 + 16)

            @block.scalar
            def _(act):
                act.wait_ge(s_oh_a, 1)
                for c in range(EC):
                    nc.scalar.activation(off_b[:, c, :], iota_row[0:EP, 0:M], ACT.Square, scale=-1.0,
                                         bias=b_f[:, c:c + 1]).then_inc(s_off_b, 1)
                act.wait_ge(s_off_b, EC)
                nc.scalar.activation(oh_b[:], off_b[:], ACT.Relu, bias=1.0, scale=-1.0).then_inc(s_oh, 1)

            @block.tensor
            def _(pe):
                pe.wait_ge(s_cum, 1)
                for k in range(RBATCH):
                    if k >= 2:
                        pe.wait_ge(s_rank_used, k - 1)
                    for c in range(k * RB, min(EC, (k + 1) * RB)):
                        o = ps_u[k % 2][0:EP, (c - k * RB) * TILES:(c - k * RB + 1) * TILES]
                        h, i = divmod(c, CL)
                        earlier = ([cum[:, c - 1, :]] if i else []) + ([in_chains(h - 1)] if h else [])
                        last = nc.tensor.matmul(o, before[:], oh_a[:, c, :], start=True, stop=not earlier)
                        for part in earlier:
                            last = nc.tensor.matmul(o, ones16[:], part, start=False, stop=part is earlier[-1])
                    last.then_inc(s_rank_mm, 1)
                pe.wait_ge(s_oh, 1)
                for c in range(EC):
                    last = nc.tensor.matmul(ps_t[0:M, 0, 0:TILES], oh_b[:, c, :], oh_a[:, c, :],
                                            start=(c == 0), stop=(c == EC - 1))
                last.then_inc(s_count, 1)
                last = nc.tensor.matmul(ps_t[0:EP, 1, 0:TILES], ones16[:], in_chains(CH - 1), start=True, stop=True)
                last.then_inc(s_total, 1)
                pe.wait_ge(s_vals, 3)
                pe.wait_ge(s_oh_r, 1)
                for c in range(EC):
                    last = nc.tensor.matmul(ps_y[:, 0, 0:3 * TILES], oh_r[:, c, :],
                                            vals[:, c, :, :].rearrange("p k t -> p (k t)"),
                                            start=(c == 0), stop=(c == EC - 1))
                last.then_inc(s_lists, 1)

            @block.vector
            def _(dve):
                n = [0]

                def link(ins):
                    n[0] += 1
                    ins.then_inc(s_chain, 1)
                    dve.wait_ge(s_chain, n[0])

                V = nc.vector
                dve.wait_ge(s_iota, 1)
                V.tensor_copy(iota_row[:], iota_row_i[:])
                link(V.tensor_copy(iota_part[:], iota_part_i[:]))
                V.memset(ones16[:], 1.0)
                V.tensor_scalar(ident16[:], iota_row[:], iota_part[:], None, ALU.is_equal)
                V.tensor_scalar(ident[:], iota_row[:], iota_part[:], None, ALU.is_equal)
                V.tensor_scalar(rank8[:], iota_row[:, 0:NE], -1.0, float(NE), ALU.mult, ALU.add)
                V.tensor_scalar(before[:], iota_row[0:EP, 0:EP], iota_part[0:EP, :], None, ALU.is_gt)
                dve.wait_ge(s_edges, 32)
                V.tensor_copy(src_f, src_i[:])
                link(V.tensor_copy(dst_f, dst_i[:]))
                V.tensor_scalar(q_i[:, 0, :], dst_f, 0.5, 1.0 / TILES, ALU.add, ALU.mult)
                link(V.tensor_scalar(q_i[:, 1, :], src_f, 0.5, 1.0 / SRC_LO, ALU.add, ALU.mult))
                V.tensor_copy(q_f, q_i[:, 0, :])
                link(V.tensor_copy(hi_f, q_i[:, 1, :]))
                V.scalar_tensor_tensor(lo_f, hi_f, -float(SRC_LO), src_f, ALU.mult, ALU.add)
                link(V.scalar_tensor_tensor(r_f, q_f, -float(TILES), dst_f, ALU.mult, ALU.add))
                link(V.tensor_scalar(neg_f, r_f, 0.0, None, ALU.is_lt))
                V.scalar_tensor_tensor(a_f, neg_f, float(TILES), r_f, ALU.mult, ALU.add)
                link(V.tensor_tensor(b_f, q_f, neg_f, ALU.subtract))
                link(V.tensor_tensor(oh_a[:], a_f.unsqueeze(2).to_broadcast([EP, EC, TILES]),
                                     iota_row[0:EP, 0:TILES].unsqueeze(1).to_broadcast([EP, EC, TILES]),
                                     ALU.is_equal))
                V.tensor_scalar(b1_f, b_f, 1.0, None, ALU.add).then_inc(s_oh_a, 1)
                cum_v, oh_v = (v[:].rearrange("p (h c) t -> p h c t", h=CH) for v in (cum, oh_a))
                link(V.tensor_copy(cum_v[:, :, 0, :], oh_v[:, :, 0, :]))
                for i in range(1, CL):
                    link(V.tensor_tensor(cum_v[:, :, i, :], cum_v[:, :, i - 1, :], oh_v[:, :, i, :], ALU.add))
                for h in range(1, CH):
                    link(V.tensor_tensor(in_chains(h), in_chains(h - 1), cum[:, (h + 1) * CL - 1, :], ALU.add))
                V.engine_nop().then_inc(s_cum, 1)
                for k in range(RBATCH):
                    dve.wait_ge(s_rank_mm, k + 1)
                    c0, c1 = k * RB, min(EC, (k + 1) * RB)
                    w = c1 - c0
                    link(V.tensor_tensor(picked[:, 0:w, :], oh_a[:, c0:c1, :],
                                         ps_u[k % 2][0:EP, 0:w * TILES].rearrange("p (c t) -> p c t", c=w),
                                         ALU.mult))
                    V.engine_nop().then_inc(s_rank_used, 1)
                    link(V.tensor_reduce(rank_f[:, c0:c1], picked[:, 0:w, :], AX.X, ALU.add))
                V.tensor_tensor(oh_r[:], rank_f.unsqueeze(2).to_broadcast([EP, EC, WIN]),
                                iota_row[0:EP, 0:WIN].unsqueeze(1).to_broadcast([EP, EC, WIN]),
                                ALU.is_equal).then_inc(s_oh_r, 1)
                dve.wait_ge(s_total, 1)
                V.tensor_reduce(most[:], ps_t[0:1, 1, 0:TILES], AX.X, ALU.max)
                V.tensor_copy(row_i[:, :, 0], src_f)
                V.tensor_copy(row_i[:, :, 1], dst_f)
                V.tensor_copy(row_i[:, :, 2].bitcast(F32), b_f)
                V.scalar_tensor_tensor(pos_i[:], a_f, float(SLOTS), rank_f, ALU.mult, ALU.add).then_inc(s_most, 1)
                dve.wait_ge(s_count, 1)
                deg, half, y, u = tmp_w[0:M, 0, :], newton[0:M, 1, :], newton[0:M, 0, :], newton[0:M, 2, :]
                link(V.tensor_scalar(deg, ps_t[0:M, 0, 0:TILES], 1.0, None, ALU.add))
                V.tensor_scalar(half, deg, -0.5, None, ALU.mult)
                link(V.tensor_scalar(y.bitcast(I32), deg.bitcast(I32), -0.5, float(RSQRT_MAGIC),
                                     ALU.mult, ALU.add))
                for _i in range(4):
                    link(V.tensor_tensor(u, y, y, ALU.mult))
                    link(V.tensor_tensor(u, u, half, ALU.mult))
                    link(V.scalar_tensor_tensor(y, u, 1.5, y, ALU.add, ALU.mult))
                V.engine_nop().then_inc(s_dinv, 1)
                link(V.reciprocal(deg_inv[0:M, :], deg))
                link(V.tensor_scalar(deg_inv[0:M, :], deg_inv[0:M, :], XS, None, ALU.mult))
                dve.wait_ge(s_lists, 1)
                link(V.tensor_copy(lists[:], ps_y[:, 0, 0:3 * TILES].rearrange("p (k t) -> p k t", k=3)))
                V.scalar_tensor_tensor(win_src[:], lists[:, 0, :], float(SRC_LO), lists[:, 1, :],
                                       ALU.mult, ALU.add)
                V.tensor_scalar(win_b[:], lists[:, 2, :], -1.0, None, ALU.add)
                link(V.tensor_scalar(tmp_w[:, 1, :], lists[:, 2, :], -1.0, 0.0, ALU.add, ALU.max))
                V.scalar_tensor_tensor(win_dst[:], tmp_w[:, 1, :], float(TILES), iota_row[:, 0:TILES],
                                       ALU.mult, ALU.add)
        prep.close()

        x_in = sb("x_in", [M, GT, D], F32)
        x_e = sb("x_e", [P, GT, D], F32)
        dsd = sb("dsd", [P, GT, 2], F32)
        z = sb("z", [M, D], F32)
        z_hi = sb("z_hi", [M, 2, D], F16)
        z_lo = sb("z_lo", [M, 2, D], F16)
        ze = sb("ze", [P, D], F32)
        ze_hi = sb("ze_hi", [P, 2, D], F16)
        ze_lo = sb("ze_lo", [P, 2, D], F16)
        hit = sb("hit", [P, 2, M], F16)
        a_hi = sb("a_hi", [P, KC, P], F16)
        a_lo = sb("a_lo", [P, KC, P], F16)
        x1 = early[0:M, :].rearrange("p (t n) -> p t n", n=D)
        x2 = sb("x2", [M, D], F32)
        (xt_hi, xt_lo), (v_hi, v_lo) = (
            [m[:, i * XW:(i + 1) * XW].bitcast(F16).rearrange("p (c t n) -> p c t n", c=KC, t=GT)
             for i in range(2)] for m in (third, late))
        v_f, u_act = (late[:, 2 * XW + i * GT * M:2 * XW + (i + n) * GT * M]
                      .rearrange("p (b n) -> p b n", b=n) for i, n in ((0, 2), (2, 3)))
        gates_t = sb("gates_t", [P, GT * M], F32)
        gates_rep = sb("gates_rep", [M, GT, P], F32)
        o_st = third[0:M, 2 * XW:2 * XW + 2 * D].rearrange("p (b n) -> p b n", b=2)
        st = sb("st", [P, 2, GT, 2, 6], F32)
        mv = sb("mv", [P, 2, GT, 2], F32)
        nt = sb("nt", [P, 5, 2, GT], F32)
        st2 = sb("st2", [M, 2, 6], F32)
        mv2 = sb("mv2", [M, 2], F32)
        nt2 = sb("nt2", [M, 6], F32)
        pad = sb("pad", [1, P], F32)
        lg = sb("lg", [M, GT, 32], F32)
        rt = sb("rt", [M, 7, GT, NE], F32)
        r1 = sb("r1", [M, 6, GT], F32)
        ov_list = sb("ov_list", [P, 3], I32)
        ov_x = sb("ov_x", [P, D], F32)
        ov_dsd = sb("ov_dsd", [P, 2], F32)
        ov_st = sb("ov_st", [P, 2, 6], F32)
        ov_mv = sb("ov_mv", [P, 2], F32)
        ov_nt = sb("ov_nt", [P, 6], F32)
        ov_z = sb("ov_z", [P, D], F32)
        ov_hi = sb("ov_hi", [P, D], F16)
        ov_lo = sb("ov_lo", [P, D], F16)
        ov_hit = sb("ov_hit", [P, M], F16)
        ov_sum = sb("ov_sum", [M, D], F32)
        idx_cols = sb("idx_cols", [P, GT, 2], I32)
        half1, y1_, u1, sc1, bi1 = (nt[:, i, :, :] for i in range(5))

        s_x = [sem(f"s_xin{t}") for t in range(GT)]
        s_xe = [sem(f"s_xe{t}") for t in range(GT)]
        s_ln1 = sem("s_ln1")
        s_z = sem("s_z")
        s_zlo = sem("s_zlo")
        s_xb = sem("s_xb")
        s_t1 = sem("s_t1")
        s_ahi = sem("s_ahi")
        s_alo = sem("s_alo")
        s_y = sem("s_y")
        s_x1 = sem("s_x1")
        s_ln2 = sem("s_ln2")
        s_x2 = sem("s_x2")
        s_t2 = sem("s_t2")
        s_xthi = sem("s_xthi")
        s_xtlo = sem("s_xtlo")
        s_r = sem("s_r")
        s_lg = sem("s_lg")
        s_lmax = sem("s_lmax")
        s_exp = sem("s_exp")
        s_gates = sem("s_gates")
        s_gt = sem("s_gt")
        s_gs = sem("s_gs")
        s_u = sem("s_u")
        s_gelu = sem("s_gelu")
        s_v = sem("s_v")
        s_vhi = sem("s_vhi")
        s_vlo = sem("s_vlo")
        s_d = sem("s_d")
        s_o = sem("s_o")
        s_st = [sem(f"s_st{i}") for i in range(2)]
        s_idx = sem("s_idx")
        s_ovl = sem("s_ovl")
        s_ovx = sem("s_ovx")
        s_ovr = sem("s_ovr")
        s_ovm = sem("s_ovm")
        s_ovs = sem("s_ovs")
        s_ovp = sem("s_ovp")
        s_ovlink = sem("s_ovlink")
        s_ovz = sem("s_ovz")
        s_link = sem("s_link")

        def until(eng, sm, value):
            if isinstance(value, int) and value <= 0:
                return
            eng.wait_ge(sm, value)

        def counters(eng):
            done = eng.alloc_register(f"windows_{eng.engine.name}")
            eng.reg_mov(done, 0)
            return eng.value_load(most[0:1, 0:1], min_val=0, max_val=E), done

        def further_windows(eng, full, done, window):
            with eng.Fori(1, ROUNDS) as r:
                with eng.If(full > r * WIN):
                    window(r, eng.snap(done, min_val=0, max_val=TILES * ROUNDS))
                    eng.reg_add(done, done, 1)

        def over_groups(eng, body):
            body(0, True, False)
            with eng.Fori(1, GROUPS - 1) as g:
                body(g, False, False)
            body(GROUPS - 1, False, True)

        def x1_at(g, t):
            return x1[:, bass.ds((g % 2) * GT + t, 1), :].rearrange("p o d -> p (o d)")

        turned = ps_t[:, :, 0:3 * P].rearrange("p b (c n) -> p b c n", c=3)[:, :, :, 0:M]

        def chunks(part):
            return part.rearrange("p (b c) n -> p b c n", b=2)[:, :, :, 0:M]

        with nc.Block() as block:
            @block.sync
            def _(sp):
                for t in range(GT):
                    sp.dma_start(x_in[:, t, :], x_t[:, t, :]).then_inc(s_x[t], 16)

                def store(g, t):
                    until(sp, s_o, g * GT + t + 1)
                    sp.dma_start(out_t[:, bass.ds(g * GT + t, 1), :].rearrange("p o d -> p (o d)"),
                                 o_st[:, t % 2, :]).then_inc(s_st[t % 2], 16)

                def body(g, first, last):
                    for t in range(GT):
                        if not last:
                            until(sp, s_x1, g * GT + t + 1)
                            sp.dma_start(x_in[:, t, :],
                                         x_t[:, bass.ds((g + 1) * GT + t, 1), :].rearrange("p o d -> p (o d)")
                                         ).then_inc(s_x[t], 16)
                        if not first:
                            store(g - 1, t)

                over_groups(sp, body)
                for t in range(GT):
                    store(GROUPS - 1, t)
                for i in range(2):
                    sp.wait_ge(s_st[i], 16 * TILES // 2)

            @block.gpsimd
            def _(pool):
                def gather(g, t):
                    for o, table, side in ((x_e[:, t, :], x, 0), (dsd[:, t, 0:1], dinv_dram, 0),
                                           (dsd[:, t, 1:2], dinv_dram, 1)):
                        nc.gpsimd.indirect_dma_start(o, None, table, bass.IndirectOffsetOnAxis(
                            idx_cols[:, t, side:side + 1], 0)).then_inc(s_xe[t], 16)

                def columns(g):
                    nc.gpsimd.tensor_copy(idx_cols[:, :, 0], win_src[:, bass.ds(g * GT, GT)])
                    nc.gpsimd.tensor_copy(idx_cols[:, :, 1], win_dst[:, bass.ds(g * GT, GT)]).then_inc(s_idx, 1)
                    until(pool, s_idx, g + 1)

                full, done = counters(pool)
                nc.gpsimd.memset(pad_p[:], 0.0).then_inc(s_ovp, 1)

                def further(T):
                    def window(r, k):
                        pool.wait_ge(s_ovp, k + 1)
                        pool.wait_ge(s_ovs, k + 1)
                        pool.dma_start(ov_list[0:WIN, :], list_dram[bass.ds(T * SLOTS + r * WIN, WIN), :]
                                       ).then_inc(s_ovl, 16)
                        pool.wait_ge(s_ovl, k * 16 + 16)
                        nc.gpsimd.tensor_tensor(pad_p[:], bias_row[0:1, 0:1], bias_row[0:1, 0:1], ALU.add
                                                ).then_inc(s_ovp, 1)
                        for o, table, side in ((ov_x[:], x, 0), (ov_dsd[:, 0:1], dinv_dram, 0),
                                               (ov_dsd[:, 1:2], dinv_dram, 1)):
                            nc.gpsimd.indirect_dma_start(o, None, table, bass.IndirectOffsetOnAxis(
                                ov_list[:, side:side + 1], 0)).then_inc(s_ovx, 16)

                    with pool.If(full > WIN):
                        further_windows(pool, full, done, window)

                def all_reduce(i):
                    pool.wait_ge(s_wmax, i + 1)
                    pair = slice(2 * i, 2 * i + 2)
                    nc.gpsimd.partition_all_reduce(wabs[:, pair], wmax[:, pair], P, bass.bass_isa.ReduceOp.absmax
                                                   ).then_inc(s_wabs, 1)

                columns(0)
                for t in range(GT):
                    gather(0, t)
                    if t == 1:
                        all_reduce(0)
                further(0)

                def body(g, first, last):
                    if not last:
                        for t in range(GT):
                            until(pool, s_xe[t], 48 * (g + 1))
                        columns(g + 1)
                    for t in range(GT):
                        until(pool, s_z, g * GT + t + 1)
                        nc.gpsimd.tensor_tensor(x_in[:, t, :], x_in[:, t, :], bias_row[0:M, :],
                                                ALU.add).then_inc(s_xb, 1)
                        if not last:
                            gather(g + 1, t)
                        if first and t == 0:
                            all_reduce(1)
                        if first and t == 3:
                            pool.wait_ge(s_scaled, 1)
                            pool.wait_ge(s_whi, 3)
                            nc.gpsimd.tensor_tensor(flat(w_lo[2]), stage_proj, flat(w_hi[2]), ALU.subtract
                                                    ).then_inc(s_wlop, 1)
                        if not (last and t == GT - 1):
                            further(g * GT + t + 1)

                over_groups(pool, body)

            @block.scalar
            def _(act):
                A = nc.scalar

                def split_z(g, t):
                    T = g * GT + t
                    until(act, s_ln1, g + 1)
                    until(act, s_t1, T - 1)
                    until(act, s_zlo, T)
                    for part in (z[:], z_hi[:, t % 2, :]):
                        A.activation(part, x_in[:, t, :], ACT.Identity, bias=bi1[0:M, 0, t:t + 1],
                                     scale=sc1[0:M, 0, t:t + 1])
                    A.activation(ze[:], x_e[:, t, :], ACT.Identity, bias=bi1[:, 1, t:t + 1],
                                 scale=sc1[:, 1, t:t + 1])
                    A.activation(ze_hi[:, t % 2, :], x_e[:, t, :], ACT.Identity, bias=bi1[:, 1, t:t + 1],
                                 scale=sc1[:, 1, t:t + 1]).then_inc(s_z, 1)

                def a_high(g, t):
                    T = g * GT + t
                    until(act, s_t1, T + 1)
                    until(act, s_y, T)
                    A.activation(chunks(a_hi[:]), turned, ACT.Copy).then_inc(s_ahi, 1)

                def norm2(g, t):
                    T = g * GT + t
                    until(act, s_ln2, T + 1)
                    until(act, s_t2, T)
                    A.activation(x2[:], x1_at(g, t), ACT.Identity, bias=nt2[:, 5:6], scale=nt2[:, 4:5]
                                 ).then_inc(s_x2, 1)

                def xt_high(g, t):
                    T = g * GT + t
                    until(act, s_t2, T + 1)
                    if t == 0:
                        until(act, s_u, g * KC)
                    A.activation(chunks(xt_hi[:, :, t, :]), turned, ACT.Copy).then_inc(s_xthi, 1)

                def gelu(g, c):
                    k = g * KC + c
                    until(act, s_u, k + 1)
                    until(act, s_v, k - 2)
                    A.activation(u_act[:, c % 3, :], ps_u[(c + 1) % 2][:, 0:GT * M], ACT.Gelu_apprx_tanh,
                                 scale=inv_fc).then_inc(s_gelu, 1)

                def v_high(g, c):
                    k = g * KC + c
                    until(act, s_v, k + 1)
                    if c == 0:
                        until(act, s_d, g * GT)
                    A.activation(v_hi[:, c, :, 0:M], v_f[:, c % 2, :].rearrange("p (t n) -> p t n", t=GT),
                                 ACT.Copy).then_inc(s_vhi, 1)

                act.wait_ge(s_wscale, 1)
                A.activation(flat(w_hi[0]), stage_gnn, ACT.Copy, scale=wscale[:, C_GNN:C_GNN + 1]
                             ).then_inc(s_whi, 1)
                split_z(0, 0)
                a_high(0, 0)
                split_z(0, 1)

                def split_experts(t):
                    if t == 0:
                        act.wait_ge(s_wscale, 2)
                        A.activation(flat(w_hi[1]), stage_fc, ACT.Copy, scale=wscale[:, C_FC:C_FC + 1]
                                     ).then_inc(s_whi, 1)
                    elif t == 1:
                        A.activation(flat(w_hi[2]), stage_proj, ACT.Copy, scale=wscale[:, C_PROJ:C_PROJ + 1]
                                     ).then_inc(s_whi, 1)
                    elif t == 2:
                        act.wait_ge(s_whi, 3)
                        A.activation(stage_proj, stage_proj, ACT.Copy, scale=wscale[:, C_PROJ:C_PROJ + 1]
                                     ).then_inc(s_scaled, 1)

                def body(g, first, last):
                    for t in range(GT):
                        if t < GT - 1:
                            a_high(g, t + 1)
                        if t < GT - 2:
                            split_z(g, t + 2)
                        if t > 0:
                            xt_high(g, t - 1)
                        norm2(g, t)
                        if first:
                            split_experts(t)
                    xt_high(g, GT - 1)
                    if first:
                        act.wait_ge(s_wlop, 1)
                    gelu(g, 0)
                    if not last:
                        split_z(g + 1, 0)
                    gelu(g, 1)
                    until(act, s_lmax, g + 1)
                    A.activation(rt[:, 1, :, :], rt[:, 0, :, :], ACT.Exp).then_inc(s_exp, 1)
                    gelu(g, 2)
                    until(act, s_gt, g + 1)
                    A.activation(gates_t[:].rearrange("p (t n) -> p t n", t=GT),
                                 ps_y[:, 0, :].rearrange("p (t n) -> p t n", t=GT)[:, :, 0:M],
                                 ACT.Copy).then_inc(s_gs, 1)
                    v_high(g, 0)
                    v_high(g, 1)
                    if not last:
                        split_z(g + 1, 1)
                    gelu(g, 3)
                    v_high(g, 2)
                    gelu(g, 4)
                    if not last:
                        a_high(g + 1, 0)
                    v_high(g, 3)
                    gelu(g, 5)
                    v_high(g, 4)
                    v_high(g, 5)

                over_groups(act, body)

            @block.tensor
            def _(pe):
                MM = nc.tensor.matmul
                full, done = counters(pe)

                def window(r, k):
                    pe.wait_ge(s_ovr, k + 1)
                    for h in range(2):
                        cols = slice(h * HALF, (h + 1) * HALF)
                        MM(ps_t[0:M, h, 0:HALF], ov_hit[:], ov_hi[:, cols], start=True, stop=False)
                        last = MM(ps_t[0:M, h, 0:HALF], ov_hit[:], ov_lo[:, cols], start=False, stop=True)
                    last.then_inc(s_ovm, 1)
                    pe.wait_ge(s_ovs, k + 2)

                def further():
                    with pe.If(full > WIN):
                        further_windows(pe, full, done, window)

                def aggregate(g, t):
                    T = g * GT + t
                    until(pe, s_alo, T)
                    until(pe, s_xtlo, prior_t2(g, t))
                    if t >= 2:
                        further()
                    until(pe, s_zlo, T + 1)
                    for c in range(KC):
                        o = ps_t[:, c // 3, (c % 3) * P:(c % 3) * P + M]
                        k = slice(c * P, (c + 1) * P)
                        MM(o, z_hi[:, t % 2, k], ident16[0:M, 0:M], start=True, stop=False)
                        MM(o, z_lo[:, t % 2, k], ident16[0:M, 0:M], start=False, stop=False)
                        MM(o, ze_hi[:, t % 2, k], hit[:, t % 2, :], start=False, stop=False)
                        last = MM(o, ze_lo[:, t % 2, k], hit[:, t % 2, :], start=False, stop=True)
                    last.then_inc(s_t1, 1)

                def prior_t2(g, t):
                    return g * GT + max(t - 2, 0)

                def rows(ps, hi, lo, w, c0=0, c1=KC):
                    for c in range(c0, c1):
                        for part, wt in ((hi, w_hi[w]), (hi, w_lo[w]), (lo, w_hi[w])):
                            for h in range(2):
                                last = MM(ps[:, h, 0:HALF], part[:, c, :], wt[:, c, h * HALF:(h + 1) * HALF],
                                          start=(c == 0 and part is hi and wt is w_hi[w]),
                                          stop=(c == KC - 1 and part is lo))
                    return last

                def gnn(g, t):
                    T = g * GT + t
                    until(pe, s_alo, T + 1)
                    until(pe, s_x1, T)
                    if t == 0:
                        pe.wait_ge(s_wlo, 1)
                        until(pe, s_gs, g)
                    rows(ps_y, a_hi, a_lo, 0).then_inc(s_y, 1)

                def down(g, t, c0=0, c1=KC, ps=ps_d, behind=0):
                    T = g * GT + t
                    if t == 0:
                        pe.wait_ge(s_wlop, 1)
                        until(pe, s_vlo, g * KC + c1)
                    if c0 == 0:
                        until(pe, s_o, T - behind)
                    last = rows(ps, v_hi[:, :, t, :], v_lo[:, :, t, :], 2, c0, c1)
                    if c1 == KC:
                        last.then_inc(s_d, 1)

                def turn(g, t):
                    T = g * GT + t
                    until(pe, s_x2, T + 1)
                    until(pe, s_alo, g * GT + min(t + 3, GT))
                    until(pe, s_xtlo, T)
                    for c in range(KC):
                        last = nc.tensor.transpose(ps_t[:, c // 3, (c % 3) * P:(c % 3) * P + M],
                                                   x2[:, c * P:(c + 1) * P], ident[0:M, 0:M])
                    last.then_inc(s_t2, 1)

                def router(g, t):
                    until(pe, s_xthi, g * GT + t + 1)
                    if t == 0:
                        until(pe, s_gelu, g * KC)
                    for c in range(KC):
                        MM(ps_u[0][:, t * 32:t * 32 + 2 * NE], xt_hi[:, c, t, :], gate[:, c, :],
                           start=(c == 0), stop=(c == KC - 1))
                    if t < GT - 1:
                        router_low(g, t)

                def router_low(g, t):
                    until(pe, s_xtlo, g * GT + t + 1)
                    for c in range(KC):
                        last = MM(ps_u[0][:, t * 32 + 2 * NE:t * 32 + 3 * NE], xt_lo[:, c, t, :],
                                  gate[:, c, 0:NE], start=(c == 0), stop=(c == KC - 1))
                    if t == GT - 1:
                        last.then_inc(s_r, 1)

                def up(g, m):
                    k = g * KC + m
                    if m == 0:
                        pe.wait_ge(s_wlo, 3)
                        until(pe, s_gelu, k - 1)
                    elif m == 1:
                        until(pe, s_lg, g + 1)
                    else:
                        until(pe, s_gelu, k - 1)
                    o = ps_u[(m + 1) % 2][:, 0:GT * M]
                    n = slice(m * P, (m + 1) * P)
                    if m == 0:
                        for c in range(KC):
                            MM(o, w_hi[1][:, c, n], xt_hi[:, c, :, 0:M], start=(c == 0), stop=False)
                            MM(o, w_lo[1][:, c, n], xt_hi[:, c, :, 0:M], start=False, stop=False)
                        router_low(g, GT - 1)
                        for c in range(KC):
                            last = MM(o, w_hi[1][:, c, n], xt_lo[:, c, :, 0:M], start=False, stop=(c == KC - 1))
                    else:
                        for c in range(KC):
                            if m == 3 and c == 2:
                                turn_gates(g)
                            MM(o, w_hi[1][:, c, n], xt_hi[:, c, :, 0:M], start=(c == 0), stop=False)
                            MM(o, w_hi[1][:, c, n], xt_lo[:, c, :, 0:M], start=False, stop=False)
                            last = MM(o, w_lo[1][:, c, n], xt_hi[:, c, :, 0:M], start=False, stop=(c == KC - 1))
                    last.then_inc(s_u, 1)

                def turn_gates(g):
                    until(pe, s_gates, g + 1)
                    until(pe, s_x1, (g + 1) * GT)
                    for t in range(GT):
                        last = nc.tensor.transpose(ps_y[:, 0, t * P:t * P + M], gates_rep[:, t, :],
                                                   ident[0:M, 0:M])
                    last.then_inc(s_gt, 1)

                further()
                aggregate(0, 0)
                pe.wait_ge(s_alo, 1)
                further()

                def body(g, first, last):
                    for t in range(GT - 1):
                        gnn(g, t)
                        aggregate(g, t + 1)
                        if not first:
                            down(g - 1, t)
                        if t > 0:
                            turn(g, t - 1)
                    gnn(g, 3)
                    router(g, 0)
                    router(g, 1)
                    turn(g, 2)
                    if not first:
                        down(g - 1, 3, 0, KC - 1)
                    router(g, 2)
                    turn(g, 3)
                    if not first:
                        down(g - 1, 3, KC - 1, KC)
                    router(g, 3)
                    up(g, 0)
                    if not last:
                        further()
                    up(g, 1)
                    up(g, 2)
                    up(g, 3)
                    if not last:
                        further()
                    up(g, 4)
                    if not last:
                        aggregate(g + 1, 0)
                    up(g, 5)

                over_groups(pe, body)
                g = GROUPS - 1
                down(g, 0, 0, KC - 2)
                down(g, 0, KC - 2, KC - 1)
                down(g, 0, KC - 1, KC)
                for t in range(1, GT):
                    down(g, t, ps=(ps_d, ps_y)[t % 2], behind=1)

            @block.vector
            def _(dve):
                V = nc.vector
                n, pads = [0, 0], []

                def link(ins):
                    n[1] += 1
                    ins.then_inc(s_link, 1)
                    dve.wait_ge(s_link, n[0] + n[1])

                def stats1(g, t):
                    until(dve, s_x[t], 16 * (g + 1))
                    until(dve, s_xe[t], 48 * (g + 1))
                    for h in range(2):
                        V.bn_stats(st[0:M, 0, t, h, :], x_in[:, t, h * HALF:(h + 1) * HALF])
                        last = V.bn_stats(st[:, 1, t, h, :], x_e[:, t, h * HALF:(h + 1) * HALF])
                    return last

                def carry_wait():
                    pads.append(0)
                    V.memset(pad[:, len(pads) - 1:len(pads)], 0.0)

                def rsqrt(y, half, u, var, link, before_last=None):
                    V.tensor_scalar(half, var, EPS, -0.5, ALU.add, ALU.mult)
                    link(V.tensor_scalar(u, var, EPS, None, ALU.add))
                    link(V.tensor_scalar(y.bitcast(I32), u.bitcast(I32), -0.5, float(RSQRT_MAGIC),
                                         ALU.mult, ALU.add))
                    for _i in range(3):
                        if _i == 2 and before_last:
                            before_last()
                        if y.free_size() == 1:
                            link(V.scalar_tensor_tensor(u, y, half, y, ALU.mult, ALU.mult))
                        else:
                            link(V.tensor_tensor(u, y, y, ALU.mult))
                            link(V.tensor_tensor(u, u, half, ALU.mult))
                        link(V.scalar_tensor_tensor(y, u, 1.5, y, ALU.add, ALU.mult))

                def finish1(g, before_last=None):
                    carry_wait()
                    for t in range(GT):
                        V.bn_aggr(mv[0:M, 0, t, :], st[0:M, 0, t, :, :].rearrange("p a b -> p (a b)"))
                        last = V.bn_aggr(mv[:, 1, t, :], st[:, 1, t, :, :].rearrange("p a b -> p (a b)"))
                    link(last)
                    rsqrt(y1_, half1, u1, mv[:, :, :, 1], link, before_last)

                def scales1(g):
                    until(dve, s_z, g * GT)
                    V.tensor_tensor(sc1[0:M, 0, :], y1_[0:M, 0, :], deg_inv[0:M, bass.ds(g * GT, GT)], ALU.mult)
                    link(V.tensor_tensor(u1[:, 1, :], dsd[:, :, 0], dsd[:, :, 1], ALU.mult))
                    link(V.scalar_tensor_tensor(sc1[:, 1, :], u1[:, 1, :], XS, y1_[:, 1, :], ALU.mult, ALU.mult))
                    V.scalar_tensor_tensor(bi1, mv[:, :, :, 0], -1.0, sc1, ALU.mult, ALU.mult
                                           ).then_inc(s_ln1, 1)

                def window(r, k):
                    steps = [0]

                    def step(ins):
                        steps[0] += 1
                        ins.then_inc(s_ovlink, 1)
                        dve.wait_ge(s_ovlink, k * OV_STEPS + steps[0])

                    dve.wait_ge(s_ovx, k * 48 + 48)
                    carry_wait()
                    V.bn_stats(ov_st[:, 0, :], ov_x[:, 0:HALF])
                    step(V.bn_stats(ov_st[:, 1, :], ov_x[:, HALF:D]))
                    carry_wait()
                    step(V.bn_aggr(ov_mv[:], ov_st[:].rearrange("p a b -> p (a b)")))
                    y, half, u, norm, sc, bi = (ov_nt[:, i:i + 1] for i in range(6))
                    rsqrt(y, half, u, ov_mv[:, 1:2], step)
                    step(V.tensor_tensor(norm, ov_dsd[:, 0:1], ov_dsd[:, 1:2], ALU.mult))
                    step(V.scalar_tensor_tensor(sc, norm, XS, y, ALU.mult, ALU.mult))
                    step(V.scalar_tensor_tensor(bi, ov_mv[:, 0:1], -1.0, sc, ALU.mult, ALU.mult))
                    step(V.tensor_scalar(ov_z[:], ov_x[:], sc, bi, ALU.mult, ALU.add))
                    step(V.tensor_copy(ov_hi[:], ov_z[:]))
                    V.tensor_tensor(ov_lo[:], ov_z[:], ov_hi[:], ALU.subtract)
                    V.tensor_scalar(ov_hit[:], iota_row[:, 0:M], ov_list[:, 2:3].bitcast(F32), None, ALU.is_equal
                                    ).then_inc(s_ovr, 1)
                    dve.wait_ge(s_ovm, k + 1)
                    step(V.tensor_tensor(ov_sum[:].rearrange("p (h n) -> p h n", h=2), ps_t[0:M, :, 0:HALF],
                                         ov_sum[:].rearrange("p (h n) -> p h n", h=2), ALU.add))
                    V.memset(pad[:, P - 1:P], 0.0).then_inc(s_ovs, 1)
                    assert steps[0] == OV_STEPS, steps

                def further(T, t):
                    carry_wait()
                    with dve.If(full > WIN):
                        V.memset(ov_sum[:], 0.0).then_inc(s_ovz, 1)
                        dve.wait_ge(s_ovz, T * 3 + 1)
                        carry_wait()
                        further_windows(dve, full, done, window)
                        V.tensor_tensor(z[:], z[:], ov_sum[:], ALU.add).then_inc(s_ovz, 1)
                        dve.wait_ge(s_ovz, T * 3 + 2)
                        V.tensor_copy(z_hi[:, t % 2, :], z[:]).then_inc(s_ovz, 1)
                        dve.wait_ge(s_ovz, T * 3 + 3)
                        carry_wait()

                def low_z(g, t):
                    T = g * GT + t
                    until(dve, s_z, T + 1)
                    until(dve, s_t1, T - 1)
                    further(T, t)
                    V.tensor_tensor(z_lo[:, t % 2, :], z[:], z_hi[:, t % 2, :], ALU.subtract)
                    V.tensor_tensor(ze_lo[:, t % 2, :], ze[:], ze_hi[:, t % 2, :], ALU.subtract)
                    V.tensor_scalar(hit[:, t % 2, :], iota_row[:, 0:M], win_b[:, bass.ds(T, 1)], None, ALU.is_equal
                                    ).then_inc(s_zlo, 1)

                def a_low(g, t):
                    T = g * GT + t
                    until(dve, s_ahi, T + 1)
                    until(dve, s_y, T)
                    V.tensor_tensor(chunks(a_lo[:]), turned, chunks(a_hi[:]), ALU.subtract).then_inc(s_alo, 1)

                def residual1(g, t):
                    T = g * GT + t
                    until(dve, s_y, T + 1)
                    until(dve, s_xb, T + 1)
                    until(dve, s_x2, T - GT + 1)
                    V.scalar_tensor_tensor(x1_at(g, t).rearrange("p (h n) -> p h n", h=2), ps_y[0:M, :, 0:HALF],
                                           inv_gnn[0:M, :],
                                           x_in[:, t, :].rearrange("p (h n) -> p h n", h=2), ALU.mult, ALU.add
                                           ).then_inc(s_x1, 1)
                    until(dve, s_x1, T + 1)

                def stats2(g, t):
                    T = g * GT + t
                    carry_wait()
                    V.bn_stats(st2[:, 0, :], x1_at(g, t)[:, 0:HALF])
                    link(V.bn_stats(st2[:, 1, :], x1_at(g, t)[:, HALF:D]))
                    carry_wait()
                    link(V.bn_aggr(mv2[:], st2[:].rearrange("p a b -> p (a b)")))
                    var, y, half, u = mv2[:, 1:2], nt2[:, 0:1], nt2[:, 1:2], nt2[:, 2:3]
                    rsqrt(y, half, u, var, link)
                    until(dve, s_x2, T)
                    link(V.tensor_scalar(nt2[:, 4:5], y, XS, None, ALU.mult))
                    V.scalar_tensor_tensor(nt2[:, 5:6], mv2[:, 0:1], -1.0, nt2[:, 4:5], ALU.mult, ALU.mult
                                           ).then_inc(s_ln2, 1)

                def xt_low(g, t):
                    T = g * GT + t
                    until(dve, s_xthi, T + 1)
                    V.tensor_tensor(chunks(xt_lo[:, :, t, :]), turned, chunks(xt_hi[:, :, t, :]), ALU.subtract
                                    ).then_inc(s_xtlo, 1)

                def output(g, t, ps=ps_d):
                    T = g * GT + t
                    until(dve, s_d, T + 1)
                    until(dve, s_st[t % 2], (g * (GT // 2) + t // 2) * 16)
                    V.scalar_tensor_tensor(o_st[:, t % 2, :].rearrange("p (h n) -> p h n", h=2),
                                           ps[0:M, :, 0:HALF], inv_out[0:M, :],
                                           x1_at(g, t).rearrange("p (h n) -> p h n", h=2), ALU.mult, ALU.add
                                           ).then_inc(s_o, 1)

                def take_logits(g):
                    until(dve, s_r, g + 1)
                    until(dve, s_exp, g)
                    V.tensor_scalar(lg[:, :, 0:3 * NE],
                                    ps_u[0][0:M, 0:GT * 32].rearrange("p (t n) -> p t n", t=GT)[:, :, 0:3 * NE],
                                    inv_gate[0:M, :], None, ALU.mult).then_inc(s_lg, 1)

                def logits(g):
                    until(dve, s_lg, g + 1)
                    link(V.tensor_tensor(lg[:, :, 0:NE], lg[:, :, 0:NE], lg[:, :, NE:2 * NE], ALU.add))
                    link(V.tensor_tensor(lg[:, :, 0:NE], lg[:, :, 0:NE], lg[:, :, 2 * NE:3 * NE], ALU.add))
                    link(V.tensor_reduce(r1[:, 0, :], lg[:, :, 0:NE], AX.X, ALU.max))
                    V.tensor_tensor(rt[:, 0, :, :], lg[:, :, 0:NE],
                                    r1[:, 0, :].unsqueeze(2).to_broadcast([M, GT, NE]), ALU.subtract
                                    ).then_inc(s_lmax, 1)
                    until(dve, s_lmax, g + 1)

                L, EX, K, S1, L2, S2, G = (rt[:, i, :, :] for i in range(7))

                def wide(v):
                    return v.unsqueeze(2).to_broadcast([M, GT, NE])

                def top2():
                    r8 = rank8[0:M, :].unsqueeze(1).to_broadcast([M, GT, NE])
                    link(V.scalar_tensor_tensor(K, L, 0.0, r8, ALU.is_equal, ALU.mult))
                    link(V.tensor_reduce(r1[:, 1, :], K, AX.X, ALU.max))
                    link(V.tensor_tensor(S1, K, wide(r1[:, 1, :]), ALU.is_equal))
                    link(V.scalar_tensor_tensor(L2, S1, -3.0e38, L, ALU.mult, ALU.add))
                    link(V.tensor_reduce(r1[:, 2, :], L2, AX.X, ALU.max))
                    link(V.tensor_tensor(K, L2, wide(r1[:, 2, :]), ALU.is_equal))
                    link(V.tensor_tensor(K, K, r8, ALU.mult))
                    link(V.tensor_reduce(r1[:, 3, :], K, AX.X, ALU.max))
                    link(V.tensor_tensor(S2, K, wide(r1[:, 3, :]), ALU.is_equal))
                    link(V.tensor_tensor(S1, S1, S2, ALU.add))

                def gates(g):
                    until(dve, s_exp, g + 1)
                    link(V.tensor_tensor(G, EX, S1, ALU.mult))
                    link(V.tensor_reduce(r1[:, 4, :], G, AX.X, ALU.add))
                    link(V.reciprocal(r1[:, 5, :], r1[:, 4, :]))
                    link(V.tensor_tensor(G, G, wide(r1[:, 5, :]), ALU.mult))
                    until(dve, s_gt, g)
                    V.tensor_scalar(gates_rep[:].rearrange("p t (r e) -> p t r e", e=NE),
                                    G.unsqueeze(2).to_broadcast([M, GT, P // NE, NE]),
                                    v_scale[0:M, :], None, ALU.mult).then_inc(s_gates, 1)

                def gated(g, c):
                    k = g * KC + c
                    until(dve, s_gelu, k + 1)
                    if c == 0:
                        until(dve, s_gs, g + 1)
                    until(dve, s_vlo, k - 1)
                    V.tensor_tensor(v_f[:, c % 2, :], u_act[:, c % 3, :], gates_t[:], ALU.mult).then_inc(s_v, 1)

                def low_v(g, c):
                    k = g * KC + c
                    until(dve, s_vhi, k + 1)
                    V.tensor_tensor(v_lo[:, c, :, 0:M], v_f[:, c % 2, :].rearrange("p (t n) -> p t n", t=GT),
                                    v_hi[:, c, :, 0:M], ALU.subtract).then_inc(s_vlo, 1)

                full, done = counters(dve)
                V.memset(mv[:], 1.0)
                V.memset(pad[:, P - 1:P], 0.0).then_inc(s_ovs, 1)
                for part in (a_hi, a_lo):
                    V.memset(part[:, :, M:P], 0.0)
                link(V.memset(nt[:], 1.0))
                dve.wait_ge(s_w[C_GATE], 16)
                V.tensor_reduce(wmax[:, C_GATE:C_GATE + 1], gate_f[:], AX.XY, ALU.max, apply_absolute_value=True)
                dve.wait_ge(s_w[C_GNN], 16)
                V.tensor_reduce(wmax[:, C_GNN:C_GNN + 1], stage_gnn, AX.X, ALU.max, apply_absolute_value=True
                                ).then_inc(s_wmax, 1)

                def low_w(i, c, part, c0=0, c1=KC):
                    n_low[0] += 1
                    dve.wait_ge(s_whi, i + 1)
                    V.scalar_tensor_tensor(flat(w_lo[i])[:, c0 * D:c1 * D], part[:, c0 * D:c1 * D],
                                           wscale[:, c:c + 1], flat(w_hi[i])[:, c0 * D:c1 * D],
                                           ALU.mult, ALU.subtract).then_inc(s_wlo, 1)
                    dve.wait_ge(s_wlo, n_low[0])

                n_low = [0]

                def largest(c, part):
                    dve.wait_ge(s_w[c], 16)
                    return V.tensor_reduce(wmax[:, c:c + 1], part, AX.X, ALU.max, apply_absolute_value=True)

                stats1(0, 0)
                dve.wait_ge(s_wabs, 1)
                scale_of(link, C_GNN, C_GATE + 1)
                V.engine_nop().then_inc(s_wscale, 1)
                link(V.tensor_scalar(gate[:, :, 0:NE], gate_f[:], wscale[:, C_GATE:C_GATE + 1], None, ALU.mult))
                V.scalar_tensor_tensor(gate[:, :, NE:2 * NE], gate_f[:], wscale[:, C_GATE:C_GATE + 1],
                                       gate[:, :, 0:NE], ALU.mult, ALU.subtract)
                for t in range(1, GT):
                    last = stats1(0, t)
                link(last)
                finish1(0)
                scales1(0)
                low_w(0, C_GNN, stage_gnn)
                for part in (xt_hi, xt_lo):
                    V.memset(part[:, :, :, M:P], 0.0)
                low_z(0, 0)
                largest(C_PROJ, stage_proj)
                a_low(0, 0)
                largest(C_FC, stage_fc).then_inc(s_wmax, 1)
                low_z(0, 1)
                dve.wait_ge(s_wabs, 2)
                scale_of(link, C_FC, C_PROJ + 1)
                V.engine_nop().then_inc(s_wscale, 1)
                V.tensor_scalar(v_scale.bitcast(I32), wexp[:, C_FC:C_FC + 1], -1.0, (254 + 4) * float(2 ** 23),
                                ALU.mult, ALU.add)
                V.tensor_scalar(un_fc.bitcast(I32), wexp[:, C_FC:C_FC + 1], -4 * float(2 ** 23), None, ALU.add)
                link(V.tensor_scalar(un_proj.bitcast(I32), wexp[:, C_PROJ:C_PROJ + 1], -W_LOG * float(2 ** 23),
                                     None, ALU.add))
                V.tensor_tensor(inv_out, un_fc, un_proj, ALU.mult)
                n_prologue = n[1]
                counted = []

                def body(g, first, last):
                    n[0], n[1] = n_prologue + g * per_group, 0
                    for t in range(GT):
                        residual1(g, t)
                        if t < GT - 1:
                            a_low(g, t + 1)
                        stats2(g, t)
                        if t < GT - 1 and not first:
                            output(g - 1, t)
                        if t > 0:
                            xt_low(g, t - 1)
                        if t < GT - 2:
                            low_z(g, t + 2)
                        if not last:
                            sums = stats1(g + 1, t)
                        if first and t == 1:
                            low_w(1, C_FC, stage_fc, 0, 1)
                        if first and t == 2:
                            low_w(1, C_FC, stage_fc, 1, KC)
                    xt_low(g, GT - 1)
                    if not last:
                        link(sums)
                        finish1(g + 1, lambda: take_logits(g))
                        scales1(g + 1)
                    else:
                        take_logits(g)
                    logits(g)
                    top2()
                    if not last:
                        low_z(g + 1, 0)
                    gates(g)
                    if not first:
                        output(g - 1, GT - 1)
                    if first:
                        dve.wait_ge(s_wlop, 1)
                        for part in (v_hi, v_lo):
                            V.memset(part[:, :, :, M:P], 0.0)
                    gated(g, 0)
                    gated(g, 1)
                    low_v(g, 0)
                    gated(g, 2)
                    low_v(g, 1)
                    if not last:
                        low_z(g + 1, 1)
                    gated(g, 3)
                    low_v(g, 2)
                    if not last:
                        a_low(g + 1, 0)
                    gated(g, 4)
                    low_v(g, 3)
                    gated(g, 5)
                    low_v(g, 4)
                    low_v(g, 5)
                    counted.append(n[1])

                per_group = 76
                over_groups(dve, body)
                assert counted[0] == counted[1] == per_group, counted
                for t in range(GT):
                    output(GROUPS - 1, t, (ps_d, ps_y)[t % 2])


def _list_rows(nodes, edges, window=128):
    return nodes // 125 * (-(-edges // window) * window)


_INS = ["x", "src", "dst", "L0_gnn_W", "L0_gnn_b", "L0_ffn_w_fc", "L0_ffn_w_proj", "L0_ffn_w_gate"]


def kernel(**inputs):
    import numpy as _np
    import concourse.bacc as _bacc
    from concourse import mybir as _mybir
    from concourse.bass_utils import run_bass_kernel_spmd as _run

    nc = _bacc.Bacc("TRN2", target_bir_lowering=False, num_devices=1)
    arrays, args = {}, []
    for name in _INS:
        a = _np.ascontiguousarray(inputs[name])
        if name == "L0_ffn_w_proj":
            ff, d = a.shape
            ne = inputs["L0_ffn_w_gate"].shape[1]
            a = _np.ascontiguousarray(a.reshape(ff // ne, d, ne).transpose(0, 2, 1).reshape(ff, d))
        arrays[f"in_{name}"] = a
        args.append(nc.dram_tensor(f"in_{name}", a.shape, _mybir.dt.from_np(a.dtype), kind="ExternalInput").ap())
    n, d = inputs["x"].shape
    args.append(nc.dram_tensor("out", (n, d), _mybir.dt.float32, kind="ExternalOutput").ap())
    args.append(nc.dram_tensor("dinv", (n, 1), _mybir.dt.float32, kind="Internal").ap())
    args.append(nc.dram_tensor("edges", (_list_rows(n, inputs["src"].shape[0]), 3), _mybir.dt.int32,
                               kind="Internal").ap())
    gnn_moe_ffn_kernel(nc, *args)
    r = _run(nc, [arrays], core_ids=[0])
    return r.results[0]["out"]
```
